# Optimizing a Trainium2 kernel written in Bass

```python
import numpy as np
import jax
import jax.numpy as jnp

def _softmax(x, axis=-1):
    return jax.nn.softmax(x, axis=axis)

def _gelu(x):
    return jax.nn.gelu(x, approximate=True)

def _silu(x):
    return jax.nn.silu(x)

def _sigmoid(x):
    return jax.nn.sigmoid(x)

def _layernorm(x, axis=-1, eps=1e-05):
    m = jnp.mean(x, axis=axis, keepdims=True)
    v = jnp.var(x, axis=axis, keepdims=True)
    return (x - m) / jnp.sqrt(v + eps)

def _scatter_add(tgt, idx, src, axis=0):
    return tgt.at[idx].add(src)

def _segment_sum(src, seg, n):
    return jax.ops.segment_sum(src, seg, n)
kernel_name = 'mk_cond_seq_d2_seqx_r4_e12c2b'

def setup_inputs(seed: int=0):
    np.random.seed(seed)
    _w = jnp.asarray

    def _rec_inputs():
        import jax
        import jax.numpy as jnp
        _rk = jax.random.key(seed)
        x = 1.648e-05 + 1 * jax.random.normal(jax.random.fold_in(_rk, 1), (8, 512, 288), jnp.float32)
        _lenS = 512 - jax.random.randint(jax.random.fold_in(_rk, 7), (8,), 0, max(1, 512 // 4) + 1, jnp.int32)
        _lenS2 = 512 - jax.random.randint(jax.random.fold_in(_rk, 8), (8,), 0, max(1, 512 // 4) + 1, jnp.int32)
        cond_1152 = 0.00914911 + 1.00357 * jax.random.normal(jax.random.fold_in(_rk, 11), (8, 288), jnp.float32)
        return (x, cond_1152)
    x, cond_1152 = _rec_inputs()

    def _L0_cond_setup():
        import jax, jax.numpy as jnp
        import numpy as np
        B, L, C = (8, 256, 288)
        H = 16
        D = C // H
        FF = int(C * 4.0)
        EPS = 1e-06

        def _layernorm(x):
            mu = jnp.mean(x, axis=-1, keepdims=True)
            var = jnp.mean(jnp.square(x - mu), axis=-1, keepdims=True)
            return (x - mu) * jax.lax.rsqrt(var + EPS)

        def _modulate(x, shift, scale):
            return x * (1.0 + scale) + shift

        def _attention(h, W_qkv, b_qkv, W_proj, b_proj):
            b, l, c = h.shape
            qkv = h @ W_qkv + b_qkv
            qkv = qkv.reshape(b, l, 3, H, D)
            q, k, v = (qkv[:, :, 0], qkv[:, :, 1], qkv[:, :, 2])
            scale = D ** (-0.5)
            scores = jnp.einsum('blhd,bmhd->bhlm', q * scale, k)
            attn = jax.nn.softmax(scores, axis=-1)
            o = jnp.einsum('bhlm,bmhd->blhd', attn, v).reshape(b, l, c)
            return o @ W_proj + b_proj
        key = jax.random.key(seed)
        ks = jax.random.split(key, 12)
        s = 0.02
        return {'x': jax.random.normal(ks[0], (B, L, C), jnp.float32), 'c': jax.random.normal(ks[1], (B, 1, C), jnp.float32), 'W_qkv': jax.random.normal(ks[2], (C, 3 * C), jnp.float32) * s, 'b_qkv': jnp.zeros((3 * C,), jnp.float32), 'W_proj': jax.random.normal(ks[3], (C, C), jnp.float32) * s, 'b_proj': jnp.zeros((C,), jnp.float32), 'W_fc1': jax.random.normal(ks[4], (C, FF), jnp.float32) * s, 'b_fc1': jnp.zeros((FF,), jnp.float32), 'W_fc2': jax.random.normal(ks[5], (FF, C), jnp.float32) * s, 'b_fc2': jnp.zeros((C,), jnp.float32), 'W_ada': jax.random.normal(ks[6], (C, 6 * C), jnp.float32) * s, 'b_ada': jnp.zeros((6 * C,), jnp.float32)}
    _L0_cond_all = _L0_cond_setup()
    _L0_cond_in = {k: v for k, v in _L0_cond_all.items() if k in ('W_qkv', 'b_qkv', 'W_proj', 'b_proj', 'W_fc1', 'b_fc1', 'W_fc2', 'b_fc2', 'W_ada', 'b_ada')}
    del _L0_cond_all

    def _L1_cond_setup():
        import jax, jax.numpy as jnp
        import numpy as np
        B, S, D = (8, 256, 288)
        H = 16
        HD = D // H
        HID = int(D * 4.0)
        LN_EPS = 1e-05

        def layer_norm(x, w, b):
            m = jnp.mean(x, axis=-1, keepdims=True)
            v = jnp.mean(jnp.square(x - m), axis=-1, keepdims=True)
            return (x - m) * jax.lax.rsqrt(v + LN_EPS) * w + b

        def modulate(x, shift, scale):
            return x * (1.0 + scale[:, None, :]) + shift[:, None, :]

        def attention(x, wq, wk, wv, wo, wo_b):
            b, s, d = x.shape
            q = (x @ wq).reshape(b, s, H, HD).transpose(0, 2, 1, 3)
            k = (x @ wk).reshape(b, s, H, HD).transpose(0, 2, 1, 3)
            v = (x @ wv).reshape(b, s, H, HD).transpose(0, 2, 1, 3)
            scale = 1.0 / np.sqrt(HD).astype(np.float32)
            att = jnp.einsum('bhqd,bhkd->bhqk', q, k) * scale
            att = jax.nn.softmax(att, axis=-1)
            out = jnp.einsum('bhqk,bhkd->bhqd', att, v)
            out = out.transpose(0, 2, 1, 3).reshape(b, s, d)
            return out @ wo + wo_b
        key = jax.random.key(seed)
        ks = jax.random.split(key, 16)
        s = 0.02
        return {'x': jax.random.normal(ks[0], (B, S, D), jnp.float32), 'c': jax.random.normal(ks[1], (B, D), jnp.float32), 'ln1_w': jnp.ones((D,), jnp.float32), 'ln1_b': jnp.zeros((D,), jnp.float32), 'wq': jax.random.normal(ks[2], (D, D), jnp.float32) * s, 'wk': jax.random.normal(ks[3], (D, D), jnp.float32) * s, 'wv': jax.random.normal(ks[4], (D, D), jnp.float32) * s, 'wo': jax.random.normal(ks[5], (D, D), jnp.float32) * s, 'wo_b': jnp.zeros((D,), jnp.float32), 'ln2_w': jnp.ones((D,), jnp.float32), 'ln2_b': jnp.zeros((D,), jnp.float32), 'fc1_w': jax.random.normal(ks[6], (D, HID), jnp.float32) * s, 'fc1_b': jnp.zeros((HID,), jnp.float32), 'fc2_w': jax.random.normal(ks[7], (HID, D), jnp.float32) * s, 'fc2_b': jnp.zeros((D,), jnp.float32), 'ada_w': jax.random.normal(ks[8], (D, 6 * D), jnp.float32) * s, 'ada_b': jnp.zeros((6 * D,), jnp.float32)}
    _L1_cond_all = _L1_cond_setup()
    _L1_cond_in = {k: v for k, v in _L1_cond_all.items() if k in ('ln1_w', 'ln1_b', 'wq', 'wk', 'wv', 'wo', 'wo_b', 'ln2_w', 'ln2_b', 'fc1_w', 'fc1_b', 'fc2_w', 'fc2_b', 'ada_w', 'ada_b')}
    del _L1_cond_all
    return {'x': x, 'cond_1152': cond_1152, 'L0_cond_W_qkv': _L0_cond_in['W_qkv'], 'L0_cond_b_qkv': _L0_cond_in['b_qkv'], 'L0_cond_W_proj': _L0_cond_in['W_proj'], 'L0_cond_b_proj': _L0_cond_in['b_proj'], 'L0_cond_W_fc1': _L0_cond_in['W_fc1'], 'L0_cond_b_fc1': _L0_cond_in['b_fc1'], 'L0_cond_W_fc2': _L0_cond_in['W_fc2'], 'L0_cond_b_fc2': _L0_cond_in['b_fc2'], 'L0_cond_W_ada': _L0_cond_in['W_ada'], 'L0_cond_b_ada': _L0_cond_in['b_ada'], 'L1_cond_ln1_w': _L1_cond_in['ln1_w'], 'L1_cond_ln1_b': _L1_cond_in['ln1_b'], 'L1_cond_wq': _L1_cond_in['wq'], 'L1_cond_wk': _L1_cond_in['wk'], 'L1_cond_wv': _L1_cond_in['wv'], 'L1_cond_wo': _L1_cond_in['wo'], 'L1_cond_wo_b': _L1_cond_in['wo_b'], 'L1_cond_ln2_w': _L1_cond_in['ln2_w'], 'L1_cond_ln2_b': _L1_cond_in['ln2_b'], 'L1_cond_fc1_w': _L1_cond_in['fc1_w'], 'L1_cond_fc1_b': _L1_cond_in['fc1_b'], 'L1_cond_fc2_w': _L1_cond_in['fc2_w'], 'L1_cond_fc2_b': _L1_cond_in['fc2_b'], 'L1_cond_ada_w': _L1_cond_in['ada_w'], 'L1_cond_ada_b': _L1_cond_in['ada_b']}

def reference(x, cond_1152, L0_cond_W_qkv, L0_cond_b_qkv, L0_cond_W_proj, L0_cond_b_proj, L0_cond_W_fc1, L0_cond_b_fc1, L0_cond_W_fc2, L0_cond_b_fc2, L0_cond_W_ada, L0_cond_b_ada, L1_cond_ln1_w, L1_cond_ln1_b, L1_cond_wq, L1_cond_wk, L1_cond_wv, L1_cond_wo, L1_cond_wo_b, L1_cond_ln2_w, L1_cond_ln2_b, L1_cond_fc1_w, L1_cond_fc1_b, L1_cond_fc2_w, L1_cond_fc2_b, L1_cond_ada_w, L1_cond_ada_b):
    import jax
    import jax.numpy as jnp

    def _L0_cond_ref(x, c, W_qkv, b_qkv, W_proj, b_proj, W_fc1, b_fc1, W_fc2, b_fc2, W_ada, b_ada):
        import jax, jax.numpy as jnp
        import numpy as np
        B, L, C = (8, 256, 288)
        H = 16
        D = C // H
        FF = int(C * 4.0)
        EPS = 1e-06

        def _layernorm(x):
            mu = jnp.mean(x, axis=-1, keepdims=True)
            var = jnp.mean(jnp.square(x - mu), axis=-1, keepdims=True)
            return (x - mu) * jax.lax.rsqrt(var + EPS)

        def _modulate(x, shift, scale):
            return x * (1.0 + scale) + shift

        def _attention(h, W_qkv, b_qkv, W_proj, b_proj):
            b, l, c = h.shape
            qkv = h @ W_qkv + b_qkv
            qkv = qkv.reshape(b, l, 3, H, D)
            q, k, v = (qkv[:, :, 0], qkv[:, :, 1], qkv[:, :, 2])
            scale = D ** (-0.5)
            scores = jnp.einsum('blhd,bmhd->bhlm', q * scale, k)
            attn = jax.nn.softmax(scores, axis=-1)
            o = jnp.einsum('bhlm,bmhd->blhd', attn, v).reshape(b, l, c)
            return o @ W_proj + b_proj
        ada = jax.nn.silu(c) @ W_ada + b_ada
        shift_msa, scale_msa, gate_msa, shift_mlp, scale_mlp, gate_mlp = jnp.split(ada, 6, axis=-1)
        h = _modulate(_layernorm(x), shift_msa, scale_msa)
        x = x + gate_msa * _attention(h, W_qkv, b_qkv, W_proj, b_proj)
        h = _modulate(_layernorm(x), shift_mlp, scale_mlp)
        mlp = jax.nn.gelu(h @ W_fc1 + b_fc1, approximate=True) @ W_fc2 + b_fc2
        x = x + gate_mlp * mlp
        return x

    def _L1_cond_ref(x, c, ln1_w, ln1_b, wq, wk, wv, wo, wo_b, ln2_w, ln2_b, fc1_w, fc1_b, fc2_w, fc2_b, ada_w, ada_b):
        import jax, jax.numpy as jnp
        import numpy as np
        B, S, D = (8, 256, 288)
        H = 16
        HD = D // H
        HID = int(D * 4.0)
        LN_EPS = 1e-05

        def layer_norm(x, w, b):
            m = jnp.mean(x, axis=-1, keepdims=True)
            v = jnp.mean(jnp.square(x - m), axis=-1, keepdims=True)
            return (x - m) * jax.lax.rsqrt(v + LN_EPS) * w + b

        def modulate(x, shift, scale):
            return x * (1.0 + scale[:, None, :]) + shift[:, None, :]

        def attention(x, wq, wk, wv, wo, wo_b):
            b, s, d = x.shape
            q = (x @ wq).reshape(b, s, H, HD).transpose(0, 2, 1, 3)
            k = (x @ wk).reshape(b, s, H, HD).transpose(0, 2, 1, 3)
            v = (x @ wv).reshape(b, s, H, HD).transpose(0, 2, 1, 3)
            scale = 1.0 / np.sqrt(HD).astype(np.float32)
            att = jnp.einsum('bhqd,bhkd->bhqk', q, k) * scale
            att = jax.nn.softmax(att, axis=-1)
            out = jnp.einsum('bhqk,bhkd->bhqd', att, v)
            out = out.transpose(0, 2, 1, 3).reshape(b, s, d)
            return out @ wo + wo_b
        mod = jax.nn.silu(c) @ ada_w + ada_b
        sh_msa, sc_msa, g_msa, sh_mlp, sc_mlp, g_mlp = jnp.split(mod, 6, axis=1)
        h = modulate(layer_norm(x, ln1_w, ln1_b), sh_msa, sc_msa)
        x = x + g_msa[:, None, :] * attention(h, wq, wk, wv, wo, wo_b)
        h = modulate(layer_norm(x, ln2_w, ln2_b), sh_mlp, sc_mlp)
        h = jax.nn.gelu(h @ fc1_w + fc1_b, approximate=False) @ fc2_w + fc2_b
        x = x + g_mlp[:, None, :] * h
        return x
    x = _L0_cond_ref(x, cond_1152[:, None, :], L0_cond_W_qkv, L0_cond_b_qkv, L0_cond_W_proj, L0_cond_b_proj, L0_cond_W_fc1, L0_cond_b_fc1, L0_cond_W_fc2, L0_cond_b_fc2, L0_cond_W_ada, L0_cond_b_ada)
    x = _L1_cond_ref(x, cond_1152, L1_cond_ln1_w, L1_cond_ln1_b, L1_cond_wq, L1_cond_wk, L1_cond_wv, L1_cond_wo, L1_cond_wo_b, L1_cond_ln2_w, L1_cond_ln2_b, L1_cond_fc1_w, L1_cond_fc1_b, L1_cond_fc2_w, L1_cond_fc2_b, L1_cond_ada_w, L1_cond_ada_b)
    return x

_drawn_inputs = setup_inputs


def setup_inputs(seed=0):
    import zlib

    import numpy as np

    out = dict(_drawn_inputs(seed))
    spreads = {'L0_cond_b_qkv': (0.0, 0.8),
     'L0_cond_b_proj': (0.0, 0.364),
     'L0_cond_b_fc1': (0.0, 0.8),
     'L0_cond_b_fc2': (0.0, 0.363),
     'L0_cond_b_ada': (0.0, 0.395),
     'L1_cond_ln1_w': (1.0, 0.6),
     'L1_cond_ln1_b': (0.0, 0.8),
     'L1_cond_wo_b': (0.0, 1.767),
     'L1_cond_ln2_w': (1.0, 0.6),
     'L1_cond_ln2_b': (0.0, 2.0),
     'L1_cond_fc1_b': (0.0, 2.0),
     'L1_cond_fc2_b': (0.0, 1.989),
     'L1_cond_ada_b': (0.0, 0.411)}
    factors = {'L0_cond_W_qkv': 8.0,
     'L0_cond_W_proj': 5.688,
     'L1_cond_wq': 8.0,
     'L1_cond_wk': 8.0,
     'L1_cond_wv': 8.0,
     'L1_cond_wo': 8.0,
     'L1_cond_fc1_w': 4.476}
    for name, (base, spread) in spreads.items():
        noise = np.random.default_rng([zlib.crc32(name.encode()), seed]).standard_normal(out[name].shape)
        drawn = base * np.exp(spread * noise) if base else spread * noise
        out[name] = jnp.asarray(drawn.astype(out[name].dtype))
    for name, factor in factors.items():
        out[name] = (out[name] * factor).astype(out[name].dtype)
    return out
```

```python
import numpy as np
import concourse.bass as bass
from concourse import mybir
from contextlib import ExitStack

F32 = mybir.dt.float32
F32R = mybir.dt.float32r
BF16 = mybir.dt.bfloat16
ALU = mybir.AluOpType
ACT = mybir.ActivationFunctionType
AX = mybir.AxisListType

BATCH, TOK, C = 8, 512, 288
HEADS = 16
HD = C // HEADS
FF = 4 * C
P = 128
TT = TOK // P
TAIL = C - 2 * P
CREP = 2 * P + 3 * TAIL
KT_TAIL = 3 * TAIL + 2
GROUP = 4
GROUPS = HEADS // GROUP
BLK = 7
QK_TILES = -(-2 * HEADS // BLK)
QK_ROWS = [min(BLK, 2 * HEADS - BLK * m) * HD for m in range(QK_TILES)]
PARTS = 3
Q_SLOTS = (0, 0, 1, 0, 2, 1)
K_SLOTS = (0, 1, 0, 2, 0, 1)
SLOTS = len(Q_SLOTS)
KS = SLOTS * HD
KM = KS + PARTS
VW = HD + 1
VPAD = (HEADS - 1) * VW + 32
FT = FF // P
HALF = TOK // 2
SCALE = float(HD) ** -0.5
EPS = (1e-6, 1e-5)
NS = GROUPS * TT * GROUP
AHEAD = 24
LD_STACK = 16 * 2 * SLOTS

STACK_AT = (30, 34, 50)
LN1_AT = (3, 4, 5)
TRPRE_AT = (7, 7, 8)
V_AT = (35, 36, 37, 38)
TRO_AT = (9, 9, 10)
PROJ_AT = (14, 15, 16, 17)
QK_AT = (18, 20, 22, 24, 26)
LN2_AT = (19, 20, 21)
TRPOST_AT = (24, 24, 25)
FC1_AT = ((28, 30, 31, 33, 34), (42, 44, 46, 47, 49))
GELU_AT = (36, 51)
SPLIT_AT = (39, 53)
FC2_AT = (((43, 44, 45), (48, 50, 51)), ((56, 57, 58), (59, 60, 61)))
PAIRS = (FT + 1) // 2


def lin_units(attn, prev, nxt):
    at = []
    for t in range(NS):
        for f in range(3):
            if nxt and TRPRE_AT[f] == t:
                at.append(("trpre", f))
        if t % 16 == 6 and (prev if t < 16 else attn):
            at.append(("ot", (t // 16 - 1) % GROUPS))
        if t % 16 == 9 and (attn if t < 48 else nxt):
            at.append(("mx", (t // 16 + 1) % GROUPS))
        for f in range(3):
            if prev and TRO_AT[f] == t:
                at.append(("tro", f))
        for n in range(TT):
            if nxt and V_AT[n] == t:
                at.append(("v", n))
        for n in range(TT):
            if prev and PROJ_AT[n] == t:
                at.append(("proj", n))
        for m in range(QK_TILES):
            if nxt and QK_AT[m] == t:
                at.append(("qk", m))
        for f in range(3):
            if prev and TRPOST_AT[f] == t:
                at.append(("trpost", f))
        for h in range(2):
            for u in range(PAIRS):
                if prev and FC1_AT[h][u] == t:
                    at.append(("fc1", PAIRS * h + u))
            for n in range(2):
                if prev and FC2_AT[h][n][0] == t:
                    at.append(("fc2", 2 * h + n))
    return at


PHASES = (("pro", False, False, True, -1, 1), ("first", True, False, True, 0, 1),
          ("second", True, True, True, 1, 1), ("mid", True, True, True, 2, BATCH - 3), ("last", True, True, False, BATCH - 1, 1),
          ("epi", False, True, False, BATCH, 1))
NLIN = 3


class Banks:

    def __init__(self):
        self.table, self.first = {}, {}
        used = [0] * NLIN
        for layer in range(2):
            for name, attn, prev, nxt, _, times in PHASES:
                units = lin_units(attn, prev, nxt)
                each = [sum(n % NLIN == b for n in range(len(units))) for b in range(NLIN)]
                for n, unit in enumerate(units):
                    self.table[layer, name, unit] = (n % NLIN, used[n % NLIN] + n // NLIN, each[n % NLIN])
                self.first[layer, name] = (list(used), each)
                used = [u + times * e for u, e in zip(used, each)]

    def of(self, layer, name, unit, turn):
        bank, before, each = self.table[layer, name, unit]
        return bank, before + turn * each

    def before(self, layer, name, bank, turn):
        used, each = self.first[layer, name]
        return used[bank] + turn * each[bank]


def two_layer_block(nc, x_in, cond, mask_in, ident_in, W, out):
    banks = Banks()
    x_mid = nc.dram_tensor("x_mid", (BATCH, TOK, C), F32).ap()
    qk_dram = nc.dram_tensor("qk_dram", (PARTS, 2 * HEADS, HD, TOK), BF16).ap()
    mx_dram = nc.dram_tensor("mx_dram", (GROUPS, PARTS, GROUP * TOK), BF16).ap()
    gate_dram = nc.dram_tensor("gate_dram", (2, BATCH, 3 * C), F32).ap()
    x_src = (x_in, x_mid)
    x_dst = (x_mid, out)

    ctx = ExitStack()
    with ctx:
        def sb(name, shape, dt=F32):
            return ctx.enter_context(nc.sbuf_tensor(name, list(shape), dt))

        def sem(name):
            return ctx.enter_context(nc.semaphore(name))

        w_qkv = sb("w_qkv", (P, 5, 3 * C), F32R)
        w_proj = sb("w_proj", (P, 5, C), F32R)
        w_fc1 = sb("w_fc1", (P, 5, FF), F32R)
        w_fc2 = sb("w_fc2", (P, 2, FT, C), F32R)
        q_stack = sb("q_stack", (P, GROUPS, GROUP, TOK), BF16)
        k_stack = sb("k_stack", (P, GROUPS, GROUP, TOK), BF16)
        v_next = sb("v_next", (P, TT, VPAD))
        v_cur = sb("v_cur", (P, TT, VPAD))
        probs = sb("probs", (P, 2, GROUP, TOK))
        hid = sb("hid", (P, 2, FT, HALF), F32R)
        hpre_main = hid[:, :, :, :].rearrange("p a f n -> p (a f n)")[:, 0:4 * TOK]\
            .rearrange("p (a n) -> p a n", a=4)
        hpre_tail = sb("hpre_tail", (P, TOK), F32R)
        hpost = sb("hpost", (P, 5, TOK), F32R)
        uf = sb("uf", (P, FT * HALF))
        hf = [uf[:, TOK * n:TOK * (n + 1)] for n in range(3)]
        rr_own = sb("rr_own", (P, TOK))
        rr = [uf[:, 3 * TOK:4 * TOK], rr_own[:, :]]
        wtmp = [uf[:, FF * n:FF * (n + 1)] for n in range(2)]
        qk_part = sb("qk_part", (P, 2, PARTS, TOK), BF16)
        x_pre = sb("x_pre", (P, TT, C))
        x_post = sb("x_post", (P, TT, C))
        xn = sb("xn", (P, TT, CREP))
        on = sb("on", (P, TT, CREP))
        o_sb = sb("o_sb", (P, TOK))
        gates = sb("gates", (P, 3, C))
        gated = sb("gated", (P, 2, C))
        mx = sb("mx", (P, GROUPS, 16))
        mx_part = sb("mx_part", (16, GROUPS, PARTS, P), BF16)
        mx_rest = sb("mx_rest", (16, GROUPS, P))
        osum = sb("osum", (P, TT, GROUP, 1))
        stats = sb("stats", (P, 2, TT, 6))
        mv = sb("mv", (P, 2, TT, 2))
        veps = sb("veps", (P, 2, TT))
        rstd = sb("rstd", (P, 2, TT))
        neghalf = sb("neghalf", (P, TT))
        ident = sb("ident", (P, P))
        lomask = sb("lomask", (P, 1))
        mod_a = sb("mod_a", (P, 2, 2, 3, BATCH))
        mod_b = sb("mod_b", (P, 2, 2, 3, BATCH))
        csil = x_pre[0:BATCH, :, :]
        csil_t = sb("csil_t", (P, 3, BATCH))
        prm = xn[0:10, 0, :]
        prm_t = sb("prm_t", (P, 3, 10))
        gate_sb = x_post[0:BATCH, 0:3, :]
        gate_bias = on[0:BATCH, :, :].rearrange("b t n -> b (t n)")[:, 0:3 * C].rearrange("b (a n) -> b a n", n=C)

        s1_ps = [ctx.enter_context(nc.psum_tensor(f"s1_ps{n}", [P, TOK], F32)) for n in range(2)]
        s2_ps = [ctx.enter_context(nc.psum_tensor(f"s2_ps{n}", [P, TOK], F32)) for n in range(2)]
        pv_ps = ctx.enter_context(nc.psum_tensor("pv_ps", [P, TOK], F32))
        lin_ps = [ctx.enter_context(nc.psum_tensor(f"lin_ps{n}", [P, TOK], F32)) for n in range(NLIN)]

        def per_kind(name):
            return [sem(name + "_pre"), sem(name + "_post")]

        lin_done = [sem(f"lin_done{n}") for n in range(NLIN)]
        lin_free = [sem(f"lin_free{n}") for n in range(NLIN)]
        stack_in = [sem(f"stack_in{g}") for g in range(GROUPS)]
        s1_done, mx_done = sem("s1_done"), sem("mx_done")
        mxh_done, mxm_done, mxl_done = sem("mxh_done"), sem("mxm_done"), sem("mxl_done")
        mx_out = [sem(f"mx_out{g}") for g in range(GROUPS)]
        mx_in = [sem(f"mx_in{g}") for g in range(GROUPS)]
        s2_done, exp_done = sem("s2_done"), sem("exp_done")
        pv_done, o_evac = sem("pv_done"), sem("o_evac")
        osum_done, on_ready = sem("osum_done"), sem("on_ready")
        vcur_ready = sem("vcur_ready")
        xpre_in = sem("xpre_in")
        qk_out = [sem(f"qk_out{n}") for n in range(2)]
        qkh_done, qkm_done, qkl_done = sem("qkh_done"), sem("qkm_done"), sem("qkl_done")
        stat_done, mv_done = per_kind("stat_done"), per_kind("mv_done")
        veps_done, rstd_done = per_kind("veps_done"), per_kind("rstd_done")
        norm_done, xn_ready = per_kind("norm_done"), per_kind("xn_ready")
        hi_done = per_kind("hi_done")
        lo_dve, lo_pool = per_kind("lo_dve"), per_kind("lo_pool")
        xpost_in, gates_in = sem("xpost_in"), sem("gates_in")
        tro_hi = sem("tro_hi")
        x1_done, gb_done, x2_done = sem("x1_done"), sem("gb_done"), sem("x2_done")
        gelu_done, ghi_done, glo_dve, glo_pool = sem("gelu_done"), sem("ghi_done"), sem("glo_dve"), sem("glo_pool")
        stored = sem("stored")
        const_in, const_set, cond_in = sem("const_in"), sem("const_set"), sem("cond_in")
        cond_exp, cond_step, cond_tr = sem("cond_exp"), sem("cond_step"), sem("cond_tr")
        prm_in, prm_tr, prm_done = sem("prm_in"), sem("prm_tr"), sem("prm_done")
        ada_in = [sem(f"ada_in{n}") for n in range(2)]
        ada_bias_in, ada_mm, ada_vec = sem("ada_bias_in"), sem("ada_mm"), sem("ada_vec")
        gate_step, gate_out, mod_step = sem("gate_step"), sem("gate_out"), sem("mod_step")
        w_in = [sem(f"w_in{n}") for n in range(2)]
        w_step, w_used, zero_set = sem("w_step"), sem("w_used"), sem("zero_set")

        def wait(eng, s, value):
            if not isinstance(value, int) or value > 0:
                eng.wait_ge(s, value)

        def weight_chunks(layer):
            w = W[layer]
            chunks = []
            for dst, parts, bias, n in ((w_qkv, w["qkv"], w["b_qkv"], 3 * C),
                                        (w_proj, [w["proj"]], w["b_proj"], C),
                                        (w_fc1, [w["fc1"]], w["b_fc1"], FF)):
                for k in range(3):
                    chunks.append(("k", dst, k, parts, bias, n))
            for f0 in range(0, FT, 4):
                chunks.append(("f", w_fc2, f0, [w["fc2"]], None, min(4, FT - f0)))
            return chunks

        def weight_dmas(chunk):
            kind, _, k, parts, bias, _ = chunk
            if kind == "f" or k < 2:
                return len(parts)
            return 3 * len(parts) + (2 if bias is not None else 0)

        N_CHUNKS = len(weight_chunks(0))
        QKV_SPLIT, PROJ_SPLIT, FC1_SPLIT = 3, 6, 9
        LAYERS = range(2)

        def w_count(layer, n):
            total = 0
            for la in LAYERS:
                for m, chunk in enumerate(weight_chunks(la)):
                    if (la * N_CHUNKS + m) % 2 == (layer * N_CHUNKS + n) % 2 and (la, m) <= (layer, n):
                        total += 16 * weight_dmas(chunk)
            return total

        def counts(layer, name, n):
            attns = n + 1 if name == "pro" else n
            posts = BATCH * layer if name in ("pro", "first") else n - 1
            pres = n if name == "epi" else n + 1
            return attns, posts, pres

        block = ctx.enter_context(nc.Block())

        @block.sync
        def _(sp):
            sp.dma_start(ident[:, :], ident_in).then_inc(const_in, 16)
            sp.dma_start(lomask[:, :], mask_in).then_inc(const_in, 16)
            sp.dma_start(csil[:, 0, :], cond).then_inc(cond_in, 16)
            n = 0
            for layer in LAYERS:
                w = W[layer]
                if layer:
                    sp.wait_ge(prm_done, 1)
                for a, b in ((0, C), (C, C + TAIL), (C + TAIL, CREP)):
                    src = slice(0, C) if a == 0 else slice(C - TAIL, C)
                    sp.dma_start(prm[0:6, a:b], w["b_ada"].rearrange("(r n) -> r n", n=C)[:, src]).then_inc(prm_in, 16)
                    for r, v in enumerate(w["ln"]):
                        sp.dma_start(prm[6 + r:7 + r, a:b], v.rearrange("(o n) -> o n", o=1)[:, src]).then_inc(prm_in, 16)
                for r, v in enumerate((w["b_ada"][2 * C:3 * C], w["b_ada"][5 * C:6 * C], w["b_fc2"])):
                    if layer and r == 0:
                        sp.wait_ge(gate_out, 16)
                    sp.dma_start(gate_bias[:, r, :], v.rearrange("(o n) -> o n", o=1).to_broadcast([BATCH, C])
                                 ).then_inc(ada_bias_in, 16)
                for ch in range(6):
                    if n >= 2:
                        sp.wait_ge(ada_mm, n - 1)
                    buf = wtmp[n % 2][:, 0:3 * C].rearrange("p (k n) -> p k n", k=3)
                    cols = slice(C * ch, C * ch + C)
                    sp.dma_start(buf[:, 0:2, :], w["ada"][0:2 * P, cols].rearrange("(k p) n -> p k n", p=P)).then_inc(ada_in[n % 2], 16)
                    sp.dma_start(buf[0:TAIL, 2, :], w["ada"][2 * P:C, cols]).then_inc(ada_in[n % 2], 16)
                    n += 1
                sp.wait_ge(ada_vec, 6 * (layer + 1))
                sp.dma_start(gate_dram[layer, :, :], gate_sb[:, :, :].rearrange("p a n -> p (a n)")).then_inc(gate_out, 16)
            sp.wait_ge(gate_out, 32)
            sp.wait_ge(const_set, 1)
            sp.wait_ge(ada_mm, 12)

            def load_weights(layer):
                if layer:
                    sp.wait_ge(stored, 16 * TT * BATCH)
                for n, chunk in enumerate(weight_chunks(layer)):
                    kind, _, k, parts, bias, size = chunk
                    at = layer * N_CHUNKS + n
                    if at >= 2:
                        sp.wait_ge(w_used, at - 1)
                    buf, s = wtmp[at % 2], w_in[at % 2]
                    if kind == "f":
                        sp.dma_start(buf[:, 0:size * C].rearrange("p (f n) -> p f n", n=C),
                                     parts[0][k * P:(k + size) * P, :].rearrange("(f p) n -> p f n", p=P)).then_inc(s, 16)
                        continue
                    each = size // len(parts)
                    if k == 2 and bias is None:
                        sp.wait_ge(zero_set, 1)
                    for i, part in enumerate(parts):
                        if k < 2:
                            sp.dma_start(buf[:, i * each:(i + 1) * each], part[k * P:(k + 1) * P, :]).then_inc(s, 16)
                        else:
                            for r in range(3):
                                sp.dma_start(buf[TAIL * r:TAIL * (r + 1), i * each:(i + 1) * each], part[2 * P:C, :]).then_inc(s, 16)
                    if k == 2 and bias is not None:
                        for r in range(2):
                            sp.dma_start(buf[3 * TAIL + r:3 * TAIL + r + 1, 0:size], bias.rearrange("(o n) -> o n", o=1)).then_inc(s, 16)

            def load_stack(g, n):
                wait(sp, s2_done, NS * (n - 1) + 16 * (g + 1))
                for stack, first, slots in ((q_stack, 0, Q_SLOTS), (k_stack, HEADS, K_SLOTS)):
                    for r, part in enumerate(slots):
                        heads = qk_dram[part, first + GROUP * g:first + GROUP * (g + 1), :, :]
                        sp.dma_start(stack[HD * r:HD * (r + 1), g, :, :], heads.rearrange("h d n -> d h n")).then_inc(stack_in[g], 16)

            def step(layer, name, attn, prev, nxt, n, b):
                A, Q, R = counts(layer, name, n)
                def apart():
                    sp.wait_ge(const_in, 32)

                for t in range(NS):
                    if t == 0 and nxt:
                        apart()
                        wait(sp, norm_done[0], R)
                        sp.dma_start(x_pre[:, :, :], x_src[layer][b + 1, :, :].rearrange("(t p) n -> p t n", p=P)).then_inc(xpre_in, 16)
                    if t == 0 and prev:
                        apart()
                        wait(sp, stored, 16 * TT * Q)
                        sp.dma_start(x_post[:, :, :], x_src[layer][b - 1, :, :].rearrange("(t p) n -> p t n", p=P)).then_inc(xpost_in, 16)
                        sp.dma_start(gates[:, :, :].rearrange("p a n -> p (a n)"),
                                     gate_dram[layer, b - 1, :].rearrange("(o n) -> o n", o=1).to_broadcast([P, 3 * C])).then_inc(gates_in, 16)
                    if t == 0 and attn:
                        load_stack(GROUPS - 1, A)
                    if t % 16 == 11 and (attn if t < 48 else nxt):
                        g, m = (t // 16 + 1) % GROUPS, (A if t < 48 else R)
                        sp.wait_ge(mxl_done, GROUPS * m + g + 1)
                        sp.dma_start(mx_dram[g, :, :].rearrange("a (r n) -> r a n", n=P), mx_part[:, g, :, :]).then_inc(mx_out[g], 16)
                        sp.wait_ge(mx_out[g], 16 * (m + 1))
                        sp.dma_start(q_stack[KS:KM, g, :, :], mx_dram[g, :, :].rearrange("a (h n) -> a h n", n=TOK)).then_inc(mx_in[g], 16)
                    for m in range(QK_TILES):
                        if nxt and QK_AT[m] + 2 == t:
                            rows = QK_ROWS[m]
                            if m == 0:
                                for g in range(GROUPS):
                                    wait(sp, stack_in[g], LD_STACK * R)
                            sp.wait_ge(qkl_done, QK_TILES * R + m + 1)
                            if m == QK_TILES - 1:
                                sp.wait_ge(qk_out[1], 96 * (R + 1))
                            for part in range(PARTS):
                                sp.dma_start(qk_dram[part, BLK * m:BLK * m + rows // HD, :, :].rearrange("h d n -> (h d) n"),
                                             qk_part[0:rows, m % 2, part, :]).then_inc(qk_out[m % 2], 16)
                    if t in STACK_AT and nxt:
                        if t == STACK_AT[0]:
                            sp.wait_ge(qk_out[0], 144 * (R + 1))
                        load_stack(STACK_AT.index(t), R)
                    for h in range(2):
                        for i in range(2):
                            if prev and FC2_AT[h][i][2] + 1 == t:
                                tt = 2 * h + i
                                apart()
                                sp.wait_ge(x2_done, TT * Q + tt + 1)
                                sp.dma_start(x_dst[layer][b - 1, tt * P:(tt + 1) * P, :], x_post[:, tt, :]).then_inc(stored, 16)

            for layer in LAYERS:
                load_weights(layer)
                for name, attn, prev, nxt, first, times in PHASES:
                    if times == 1:
                        step(layer, name, attn, prev, nxt, BATCH * layer + first, first)
                    else:
                        with sp.Fori(first, first + times) as b:
                            step(layer, name, attn, prev, nxt, b + BATCH * layer, b)
            sp.wait_ge(stored, 16 * TT * 2 * BATCH)

        @block.tensor
        def _(pe):
            mm, tr = nc.tensor.matmul, nc.tensor.transpose
            pe.wait_ge(const_in, 32)
            pe.wait_ge(cond_step, 3)
            for k in range(3):
                rows = P if k < 2 else TAIL
                last = tr(lin_ps[0][0:rows, BATCH * k:BATCH * (k + 1)], csil[:, 3, P * k:P * k + rows], ident[0:BATCH, 0:BATCH])
            last.then_inc(cond_tr, 1)
            pe.wait_ge(cond_step, 4)
            n = 0
            for layer in LAYERS:
                pe.wait_ge(prm_in, (16 * 3) if layer == 0 else (16 * 3 + 16 * 15))
                rows = 6 if layer == 0 else 10
                for k in range(3):
                    cols = P if k < 2 else 3 * TAIL
                    last = tr(lin_ps[1][0:cols, 16 * k:16 * k + rows], prm[0:rows, P * k:P * k + cols], ident[0:rows, 0:rows])
                last.then_inc(prm_tr, 1)
                for ch in range(6):
                    pe.wait_ge(ada_in[n % 2], 32 * (n // 2 + 1))
                    if n:
                        pe.wait_ge(ada_vec, n)
                    buf = wtmp[n % 2][:, 0:3 * C].rearrange("p (k n) -> p k n", k=3)
                    if ch in (2, 5):
                        for k in range(3):
                            rows = P if k < 2 else TAIL
                            last = mm(lin_ps[2][0:BATCH, 0:C], csil_t[0:rows, k, :], buf[0:rows, k, :], start=(k == 0), stop=(k == 2))
                    else:
                        for f in range(5):
                            cols = P if f < 2 else TAIL
                            p0 = 0 if f < 2 else TAIL * (f - 2)
                            c0 = P * min(f, 2)
                            for k in range(3):
                                rows = P if k < 2 else TAIL
                                last = mm(lin_ps[2][p0:p0 + cols, BATCH * min(f, 2):BATCH * (min(f, 2) + 1)],
                                          buf[0:rows, k, c0:c0 + cols], csil_t[0:rows, k, :], start=(k == 0), stop=(k == 2))
                    last.then_inc(ada_mm, 1)
                    n += 1

            def split_products(ps, acts, weights, tail_act, tail_weight):
                pairs = [(0, 0), (1, 1), (2, 0), (3, 1), (0, 2), (1, 3)]
                for i, (a, w) in enumerate(pairs):
                    lhs, rhs = (acts(a), weights(w))
                    mm(ps, lhs, rhs, start=(i == 0), stop=False)
                return mm(ps, tail_act, tail_weight, start=False, stop=True)

            def hp(kind, tile):
                if kind == 0:
                    return hpre_main[:, tile, :] if tile < 4 else hpre_tail[0:KT_TAIL, :]
                return hpost[:, tile, :] if tile < 4 else hpost[0:KT_TAIL, 4, :]

            pe.wait_ge(prm_done, 2)
            pe.wait_ge(ada_vec, 12)

            def step(layer, name, attn, prev, nxt, n, turn):
                A, Q, R = counts(layer, name, n)
                w0 = N_CHUNKS * layer

                def bank_of(unit):
                    bank, before = banks.of(layer, name, unit, turn)
                    wait(pe, lin_free[bank], before)
                    return lin_ps[bank], lin_done[bank]

                def pre_ready():
                    pe.wait_ge(lo_pool[0], R + 1)
                    pe.wait_ge(lo_dve[0], 2 * (R + 1))
                    pe.wait_ge(w_used, w0 + QKV_SPLIT)

                def transposes(kind, f):
                    ps, done = bank_of((("trpre", "trpost")[kind], f))
                    pe.wait_ge(xn_ready[kind], ((R, Q)[kind]) + 1)
                    cols = P if f < 2 else 3 * TAIL
                    for tt in range(TT):
                        last = tr(ps[0:cols, P * tt:P * (tt + 1)], xn[:, tt, P * f:P * f + cols], ident[:, :])
                    last.then_inc(done, 1)

                for t in range(NS):
                    g, kt, j = t // 16, (t // 4) % TT, t % 4
                    if attn:
                        if kt == 0 and j == 0:
                            pe.wait_ge(mx_in[g], 16 * (A + 1))
                        wait(pe, exp_done, NS * A + t - 1)
                        mm(s2_ps[t % 2][:, :], k_stack[0:KM, g, j, P * kt:P * (kt + 1)], q_stack[0:KM, g, j, :],
                           start=True, stop=True).then_inc(s2_done, 1)
                    s = t + AHEAD
                    if attn if s < NS else nxt:
                        g1, l1, n1 = (s // 16) % GROUPS, s % 16, (A if s < NS else R)
                        if l1 == 0:
                            pe.wait_ge(stack_in[g1], LD_STACK * (n1 + 1))
                        wait(pe, mx_done, NS * n1 + s % NS - 1)
                        qt = l1 % TT
                        mm(s1_ps[s % 2][:, :], q_stack[0:KS, g1, l1 // TT, P * qt:P * (qt + 1)], k_stack[0:KS, g1, l1 // TT, :],
                           start=True, stop=True).then_inc(s1_done, 1)
                    if t % 4 == 2 and (attn if t >= 4 else prev):
                        slot, n1 = (t // 4 - 1) % 16, A - (t < 4)
                        pg, pkt = slot // TT, slot % TT
                        pe.wait_ge(exp_done, NS * n1 + 4 * (slot + 1))
                        if pkt == 0:
                            wait(pe, o_evac, GROUPS * n1 + pg)
                        if slot == 0:
                            pe.wait_ge(vcur_ready, n1 + 1)
                        for h in range(GROUP):
                            c0 = VW * (GROUP * pg + h)
                            last = mm(pv_ps[32 * h:32 * (h + 1), :], v_cur[:, pkt, c0:c0 + 32], probs[:, slot % 2, h, :],
                                      start=(pkt == 0), stop=(pkt == TT - 1))
                        last.then_inc(pv_done, 1)
                    for f in range(3):
                        if nxt and TRPRE_AT[f] == t:
                            transposes(0, f)
                    if t % 16 == 6 and (prev if t < 16 else attn):
                        og, n1 = (t // 16 - 1) % GROUPS, A - (t < 16)
                        ps, done = bank_of(("ot", og))
                        pe.wait_ge(o_evac, GROUPS * n1 + og + 1)
                        for tt in range(TT):
                            last = tr(ps[:, P * tt:P * (tt + 1)], o_sb[:, P * tt:P * (tt + 1)], ident[:, :])
                        last.then_inc(done, 1)
                    if t % 16 == 9 and (attn if t < 48 else nxt):
                        g1, n1 = (t // 16 + 1) % GROUPS, (A if t < 48 else R)
                        ps, done = bank_of(("mx", g1))
                        pe.wait_ge(mx_done, NS * n1 + 16 * (g1 + 1))
                        tr(ps[0:16, 0:P], mx[:, g1, :], ident[:, :]).then_inc(done, 1)
                    for f in range(3):
                        if prev and TRO_AT[f] == t:
                            ps, done = bank_of(("tro", f))
                            pe.wait_ge(on_ready, Q + 1)
                            cols = P if f < 2 else 3 * TAIL
                            for tt in range(TT):
                                last = tr(ps[0:cols, P * tt:P * (tt + 1)], on[:, tt, P * f:P * f + cols], ident[:, :])
                            last.then_inc(done, 1)
                    for tt in range(TT):
                        if nxt and V_AT[tt] == t:
                            ps, done = bank_of(("v", tt))
                            pre_ready()
                            tok = slice(P * tt, P * (tt + 1))
                            split_products(ps[:, 0:C], lambda a: hp(0, a)[:, tok], lambda w: w_qkv[:, w, 2 * C:3 * C],
                                           hp(0, 4)[:, tok], w_qkv[0:KT_TAIL, 4, 2 * C:3 * C]).then_inc(done, 1)
                    for tt in range(TT):
                        if prev and PROJ_AT[tt] == t:
                            ps, done = bank_of(("proj", tt))
                            for f in range(3):
                                tro_bank, before = banks.of(layer, name, ("tro", f), turn)
                                pe.wait_ge(lin_free[tro_bank], before + 1)
                            pe.wait_ge(w_used, w0 + PROJ_SPLIT)
                            tok = slice(P * tt, P * (tt + 1))
                            split_products(ps[:, 0:C], lambda a: hp(1, a)[:, tok], lambda w: w_proj[:, w, :],
                                           hp(1, 4)[:, tok], w_proj[0:KT_TAIL, 4, :]).then_inc(done, 1)
                    for m in range(QK_TILES):
                        if nxt and QK_AT[m] == t:
                            ps, done = bank_of(("qk", m))
                            pre_ready()
                            rows = QK_ROWS[m]
                            cols = slice(BLK * HD * m, BLK * HD * m + rows)
                            pairs = [(0, 0), (1, 1), (2, 0), (3, 1), (0, 2), (1, 3)]
                            for i, (a, w) in enumerate(pairs):
                                mm(ps[0:rows, :], w_qkv[:, w, cols], hp(0, a), start=(i == 0), stop=False)
                            mm(ps[0:rows, :], w_qkv[0:KT_TAIL, 4, cols], hp(0, 4), start=False, stop=True).then_inc(done, 1)
                    for f in range(3):
                        if prev and TRPOST_AT[f] == t:
                            transposes(1, f)
                    for h in range(2):
                        tok = slice(HALF * h, HALF * (h + 1))
                        for u in range(PAIRS):
                            if prev and FC1_AT[h][u] == t:
                                ps, done = bank_of(("fc1", PAIRS * h + u))
                                pe.wait_ge(lo_pool[1], Q + 1)
                                pe.wait_ge(lo_dve[1], 2 * (Q + 1))
                                pe.wait_ge(w_used, w0 + FC1_SPLIT)
                                for f in range(2 * u, min(2 * u + 2, FT)):
                                    o = ps[:, HALF * (f % 2):HALF * (f % 2 + 1)]
                                    pairs = [(0, 0), (1, 1), (2, 0), (3, 1), (0, 2), (1, 3)]
                                    for i, (a, w) in enumerate(pairs):
                                        mm(o, w_fc1[:, w, P * f:P * (f + 1)], hp(1, a)[:, tok], start=(i == 0), stop=False)
                                    last = mm(o, w_fc1[0:KT_TAIL, 4, P * f:P * (f + 1)], hp(1, 4)[:, tok], start=False, stop=True)
                                last.then_inc(done, 1)
                        for i in range(2):
                            for c in range(3):
                                if prev and FC2_AT[h][i][c] == t:
                                    if c == 0:
                                        fc2_ps, fc2_bank = bank_of(("fc2", 2 * h + i))
                                        pe.wait_ge(w_used, w0 + N_CHUNKS)
                                    pe.wait_ge(ghi_done, 6 * Q + 3 * h + c + 1)
                                    if c == 0:
                                        pe.wait_ge(glo_pool, 2 * Q + h + 1)
                                    else:
                                        pe.wait_ge(glo_dve, 4 * Q + 2 * h + c)
                                    for f in range(3 * c, 3 * c + 3):
                                        for a, w in ((0, 0), (1, 0), (0, 1)):
                                            last = mm(fc2_ps[:, 0:C], hid[:, a, f, P * i:P * (i + 1)], w_fc2[:, w, f, :],
                                                      start=(f == 0 and a == 0 and w == 0), stop=(f == FT - 1 and w == 1))
                                    if c == 2:
                                        last.then_inc(fc2_bank, 1)

            for layer in LAYERS:
                for name, attn, prev, nxt, first, times in PHASES:
                    if times == 1:
                        step(layer, name, attn, prev, nxt, BATCH * layer + first, 0)
                    else:
                        with pe.Fori(first, first + times) as b:
                            step(layer, name, attn, prev, nxt, b + BATCH * layer, b - first)

        @block.scalar
        def _(act):
            fn = nc.scalar.activation
            gelu = (ACT.Gelu_apprx_tanh, ACT.Gelu)
            act.wait_ge(cond_in, 16)
            fn(csil[:, 1, :], csil[:, 0, :], ACT.Exp, scale=-1.0).then_inc(cond_exp, 1)
            act.wait_ge(ada_vec, 12)
            act.wait_ge(mod_step, 4)

            def step(layer, name, attn, prev, nxt, n, b, turn):
                A, Q, R = counts(layer, name, n)
                R2 = R + 1 if nxt else R

                def bank_of(unit):
                    bank, before = banks.of(layer, name, unit, turn)
                    act.wait_ge(lin_done[bank], before + 1)
                    return lin_ps[bank], lin_free[bank]

                def modulate(kind, f):
                    ps, free = bank_of((("trpre", "trpost")[kind], f))
                    rows = P if f < 2 else 3 * TAIL
                    bb = (b + 1) if kind == 0 else (b - 1)
                    fn(hf[f][0:rows, :], ps[0:rows, :], ACT.Identity, scale=mod_a[0:rows, layer, kind, f, bass.ds(bb, 1)],
                       bias=mod_b[0:rows, layer, kind, f, bass.ds(bb, 1)]).then_inc(free, 1)

                for t in range(NS):
                    if attn:
                        slot = t // 4
                        act.wait_ge(s2_done, NS * A + t + 1)
                        if t % 4 == 0:
                            wait(act, pv_done, 16 * A + slot - 1)
                        fn(probs[:, slot % 2, t % 4, :], s2_ps[t % 2][:, :], ACT.Exp, scale=SCALE).then_inc(exp_done, 1)
                    if t % 16 == 3 and (prev if t < 16 else attn):
                        og, n1 = (t // 16 - 1) % GROUPS, A - (t < 16)
                        act.wait_ge(pv_done, 16 * n1 + TT * (og + 1))
                        wait(act, osum_done, GROUPS * n1 + og)
                        fn(o_sb[:, :], pv_ps[:, :], ACT.Copy).then_inc(o_evac, 1)
                    for f in range(3):
                        if nxt and TRPRE_AT[f] + 1 == t:
                            if f == 0:
                                wait(act, glo_dve, 4 * Q)
                                wait(act, glo_pool, 2 * Q)
                                wait(act, qkl_done, QK_TILES * R)
                            modulate(0, f)
                    for f in range(3):
                        if prev and TRO_AT[f] + 1 == t:
                            ps, _ = bank_of(("tro", f))
                            rows = P if f < 2 else 3 * TAIL
                            fn(hpost[0:rows, f if f < 2 else 4, :], ps[0:rows, :], ACT.Copy).then_inc(tro_hi, 1)
                    for m in range(QK_TILES):
                        if nxt and QK_AT[m] + 1 == t:
                            ps, _ = bank_of(("qk", m))
                            rows = QK_ROWS[m]
                            wait(act, qk_out[m % 2], (144, 96)[m % 2] * R + 48 * (m // 2))
                            fn(qk_part[0:rows, m % 2, 0, :], ps[0:rows, :], ACT.Copy).then_inc(qkh_done, 1)
                    for f in range(3):
                        if prev and TRPOST_AT[f] + 1 == t:
                            if f == 0:
                                wait(act, lo_pool[0], R2)
                                wait(act, lo_dve[0], 2 * R2)
                            modulate(1, f)
                    for h in range(2):
                        for u in range(PAIRS):
                            if prev and FC1_AT[h][u] + 1 == t:
                                ps, free = bank_of(("fc1", PAIRS * h + u))
                                if u == 0 and h == 1:
                                    act.wait_ge(glo_dve, 4 * Q + 2)
                                    act.wait_ge(glo_pool, 2 * Q + 1)
                                if u == 0 and h == 0:
                                    act.wait_ge(lo_dve[1], 2 * (Q + 1))
                                    act.wait_ge(lo_pool[1], Q + 1)
                                    wait(act, qkl_done, QK_TILES * R2)
                                size = HALF * (min(2 * u + 2, FT) - 2 * u)
                                fn(uf[:, TOK * u:TOK * u + size], ps[:, 0:size], ACT.Copy).then_inc(free, 1)
                        if prev and GELU_AT[h] == t:
                            landed = {}
                            for u in range(PAIRS):
                                bank, before = banks.of(layer, name, ("fc1", PAIRS * h + u), turn)
                                landed[bank] = before + 1
                            for bank, count in landed.items():
                                act.wait_ge(lin_free[bank], count)
                            for c in range(3):
                                part = uf[:, 3 * HALF * c:3 * HALF * (c + 1)]
                                fn(part, part, gelu[layer]).then_inc(gelu_done, 1)

            for layer in LAYERS:
                for name, attn, prev, nxt, first, times in PHASES:
                    if times == 1:
                        step(layer, name, attn, prev, nxt, BATCH * layer + first, first, 0)
                    else:
                        with act.Fori(first, first + times) as b:
                            step(layer, name, attn, prev, nxt, b + BATCH * layer, b, b - first)

        @block.vector
        def _(dve):
            v = nc.vector
            v.memset(neghalf[:, :], -0.5)
            v.memset(v_next[:, :, :], 0.0).then_inc(const_set, 1)
            v.memset(k_stack[96:P, :, :, :], 1.0)
            v.memset(hpre_tail[96:P, :].bitcast(F32), 1.0)
            v.memset(hpost[96:P, 4, :].bitcast(F32), 1.0)
            dve.wait_ge(const_set, 1)
            v.memset(v_next[:, :, 0:HEADS * VW].rearrange("p t (h d) -> p t h d", d=VW)[:, :, :, HD:VW], 1.0).then_inc(const_set, 1)
            dve.wait_ge(cond_exp, 1)
            v.tensor_scalar(csil[:, 2, :], csil[:, 1, :], 1.0, None, ALU.add).then_inc(cond_step, 1)
            dve.wait_ge(cond_step, 1)
            v.reciprocal(csil[:, 1, :], csil[:, 2, :]).then_inc(cond_step, 1)
            dve.wait_ge(cond_step, 2)
            v.tensor_tensor(csil[:, 3, :], csil[:, 0, :], csil[:, 1, :], ALU.mult).then_inc(cond_step, 1)
            dve.wait_ge(cond_tr, 1)
            v.tensor_copy(csil_t[:, 0:2, :], lin_ps[0][:, 0:2 * BATCH].rearrange("p (k b) -> p k b", b=BATCH))
            v.tensor_copy(csil_t[0:TAIL, 2, :], lin_ps[0][0:TAIL, 2 * BATCH:3 * BATCH]).then_inc(cond_step, 1)
            n = 0
            for layer in LAYERS:
                rows = 6 if layer == 0 else 10
                dve.wait_ge(prm_tr, layer + 1)
                v.tensor_copy(prm_t[:, 0:2, 0:rows], lin_ps[1][:, 0:32].rearrange("p (k r) -> p k r", r=16)[:, :, 0:rows])
                v.tensor_copy(prm_t[0:3 * TAIL, 2, 0:rows], lin_ps[1][0:3 * TAIL, 32:32 + rows]).then_inc(prm_done, 1)
                dve.wait_ge(prm_done, layer + 1)
                dve.wait_ge(ada_bias_in, 48 * (layer + 1))
                for ch in range(6):
                    dve.wait_ge(ada_mm, n + 1)
                    norm = ch // 3
                    if ch % 3 == 2:
                        if layer:
                            dve.wait_ge(gate_out, 16)
                        gate = v.tensor_tensor(gate_sb[:, norm, :], lin_ps[2][0:BATCH, 0:C], gate_bias[:, norm, :], ALU.add)
                        if norm == 0:
                            gate.then_inc(ada_vec, 1)
                        else:
                            gate.then_inc(gate_step, 1)
                            dve.wait_ge(gate_step, layer + 1)
                            v.tensor_tensor(gate_sb[:, 2, :], gate_sb[:, 1, :], gate_bias[:, 2, :], ALU.mult).then_inc(ada_vec, 1)
                    else:
                        dst = mod_b if ch % 3 == 0 else mod_a
                        for f in range(3):
                            r = P if f < 2 else 3 * TAIL
                            last = v.tensor_scalar(dst[0:r, layer, norm, f, :], lin_ps[2][0:r, BATCH * f:BATCH * (f + 1)],
                                                   prm_t[0:r, f, ch:ch + 1], float(ch % 3), ALU.add, ALU.add)
                        last.then_inc(ada_vec, 1)
                        if layer and ch % 3 == 1:
                            dve.wait_ge(ada_vec, n + 1)
                            for f in range(3):
                                r = P if f < 2 else 3 * TAIL
                                a, bb = mod_a[0:r, layer, norm, f, :], mod_b[0:r, layer, norm, f, :]
                                last = v.scalar_tensor_tensor(out=bb, in0=a, scalar=prm_t[0:r, f, 7 + 2 * norm:8 + 2 * norm],
                                                              in1=bb, op0=ALU.mult, op1=ALU.add)
                            last.then_inc(mod_step, 1)
                            dve.wait_ge(mod_step, 2 * norm + 1)
                            for f in range(3):
                                r = P if f < 2 else 3 * TAIL
                                a = mod_a[0:r, layer, norm, f, :]
                                last = v.tensor_scalar(a, a, prm_t[0:r, f, 6 + 2 * norm:7 + 2 * norm], None, ALU.mult)
                            last.then_inc(mod_step, 1)
                    n += 1
            dve.wait_ge(const_in, 32)

            def split_weights(layer):
                for m, (kind, dst, k, _, bias, size) in enumerate(weight_chunks(layer)):
                    at = layer * N_CHUNKS + m
                    buf = wtmp[at % 2]
                    dve.wait_ge(w_in[at % 2], w_count(layer, m))
                    if kind == "f":
                        high, low = dst[:, 0, k:k + size, :], dst[:, 1, k:k + size, :]
                        whole = buf[:, 0:size * C].rearrange("p (f n) -> p f n", n=C)
                    elif k < 2:
                        high, low, whole = dst[:, k, 0:size], dst[:, 2 + k, 0:size], buf[:, 0:size]
                    else:
                        high = low = dst[0:KT_TAIL, 4, 0:size]
                        whole = buf[0:KT_TAIL, 0:size]
                    v.tensor_copy(high, whole).then_inc(w_step, 1)
                    dve.wait_ge(w_step, at + 1)
                    if kind == "f" or k < 2:
                        v.tensor_tensor(low, whole, high.bitcast(F32), ALU.subtract).then_inc(w_used, 1)
                    else:
                        v.scalar_tensor_tensor(out=low, in0=high.bitcast(F32), scalar=lomask[0:KT_TAIL, 0:1], in1=whole,
                                               op0=ALU.mult, op1=ALU.add).then_inc(w_used, 1)
                    if layer == 1 and m == 0:
                        dve.wait_ge(w_used, at + 1)
                        v.memset(buf[3 * TAIL:KT_TAIL, 0:3 * C], 0.0).then_inc(zero_set, 1)

            def step(layer, name, attn, prev, nxt, n, turn):
                A, Q, R = counts(layer, name, n)
                A2, Q2, R2 = A + 1 if attn else A, Q + 1 if prev else Q, R + 1 if nxt else R
                x_of = (x_pre, x_post)

                def bank_of(unit):
                    bank, before = banks.of(layer, name, unit, turn)
                    dve.wait_ge(lin_done[bank], before + 1)
                    return lin_ps[bank], lin_free[bank]

                def released(unit):
                    bank, before = banks.of(layer, name, unit, turn)
                    dve.wait_ge(lin_free[bank], before + 1)

                def norm(kind, part):
                    m = (R, Q)[kind]
                    x, st, avg = x_of[kind], stats[:, kind, :, :], mv[:, kind, :, :]
                    if part == 0:
                        if kind == 0:
                            dve.wait_ge(xpre_in, 16 * (R + 1))
                        else:
                            dve.wait_ge(x1_done, TT * (Q + 1))
                        for tt in range(TT):
                            last = v.bn_stats(st[:, tt, :], x[:, tt, :])
                        last.then_inc(stat_done[kind], 1)
                    if part == 1:
                        dve.wait_ge(const_in, 32)
                        dve.wait_ge(stat_done[kind], m + 1)
                        for tt in range(TT):
                            last = v.bn_aggr(avg[:, tt, :], st[:, tt, :])
                        last.then_inc(mv_done[kind], 1)
                        dve.wait_ge(mv_done[kind], m + 1)
                        v.tensor_scalar(veps[:, kind, :], avg[:, :, 1], EPS[layer], None, ALU.add).then_inc(veps_done[kind], 1)
                    if part == 2:
                        dve.wait_ge(rstd_done[kind], m + 1)
                        if kind == 0:
                            wait(dve, hi_done[1], 3 * Q)
                        else:
                            wait(dve, hi_done[0], 3 * R2)
                        for tt in range(TT):
                            last = v.tensor_scalar(xn[:, tt, 0:C], x[:, tt, :], avg[:, tt, 0:1], rstd[:, kind, tt:tt + 1],
                                                   ALU.subtract, ALU.mult)
                        last.then_inc(norm_done[kind], 1)
                        dve.wait_ge(norm_done[kind], m + 1)
                        repeat_tail(xn).then_inc(xn_ready[kind], 1)

                def repeat_tail(x):
                    return v.tensor_copy(x[:, :, C:CREP].rearrange("p t (a n) -> p t a n", n=TAIL),
                                         x[:, :, None, 2 * P:C].to_broadcast([P, TT, 2, TAIL]))

                def halves(kind, t, at):
                    m = (R, Q)[kind]
                    tiles = [hpre_main[:, 0, :], hpre_main[:, 1, :], hpre_tail[0:3 * TAIL, :]] if kind == 0 else \
                        [hpost[:, 0, :], hpost[:, 1, :], hpost[0:3 * TAIL, 4, :]]
                    for f in range(3):
                        if at[f] + 1 == t:
                            released((("trpre", "trpost")[kind], f))
                            rows = P if f < 2 else 3 * TAIL
                            v.tensor_copy(tiles[f], hf[f][0:rows, :]).then_inc(hi_done[kind], 1)
                    if at[2] + 2 == t:
                        low = hpre_main[:, 3, :] if kind == 0 else hpost[:, 3, :]
                        dve.wait_ge(hi_done[kind], 3 * (m + 1))
                        v.tensor_tensor(low, hf[1], tiles[1].bitcast(F32), ALU.subtract).then_inc(lo_dve[kind], 1)
                        mid = tiles[2][TAIL:2 * TAIL, :]
                        v.tensor_tensor(mid, hf[2][TAIL:2 * TAIL, :], mid.bitcast(F32), ALU.subtract).then_inc(lo_dve[kind], 1)

                def split_hidden(h, c):
                    part = uf[:, 3 * HALF * c:3 * HALF * (c + 1)].rearrange("p (f n) -> p f n", n=HALF)
                    return hid[:, 0, 3 * c:3 * c + 3, :], hid[:, 1, 3 * c:3 * c + 3, :], part

                for t in range(NS):
                    s = t + AHEAD
                    if attn if s < NS else nxt:
                        g1, l1, n1 = (s // 16) % GROUPS, s % 16, (A if s < NS else R)
                        dve.wait_ge(s1_done, NS * n1 + s % NS + 1)
                        v.tensor_reduce(mx[:, g1, l1:l1 + 1], s1_ps[s % 2][:, :], AX.X, ALU.max, negate=True).then_inc(mx_done, 1)
                    for part in range(3):
                        if nxt and LN1_AT[part] == t:
                            norm(0, part)
                    if t == 3 and attn:
                        wait(dve, pv_done, 16 * A)
                        for bank in range(NLIN):
                            wait(dve, lin_free[bank], banks.before(layer, name, bank, turn))
                        v.tensor_copy(v_cur[:, :, :], v_next[:, :, :]).then_inc(vcur_ready, 1)
                    if nxt:
                        halves(0, t, [a + 1 for a in TRPRE_AT])
                    if t % 16 == 7 and (prev if t < 16 else attn):
                        og, n1 = (t // 16 - 1) % GROUPS, A - (t < 16)
                        ps, free = bank_of(("ot", og))
                        o = ps[:, :].rearrange("p (t h c) -> p t h c", t=TT, c=32)
                        v.reciprocal(osum[:, :, :, :], o[:, :, :, HD:HD + 1]).then_inc(osum_done, 1)
                        dve.wait_ge(osum_done, GROUPS * n1 + og + 1)
                        if og == 0:
                            wait(dve, tro_hi, 3 * Q2)
                        dst = on[:, :, GROUP * HD * og:GROUP * HD * (og + 1)].rearrange("p t (h d) -> p t h d", d=HD)
                        v.tensor_tensor(dst, o[:, :, :, 0:HD], osum[:, :, :, :].to_broadcast([P, TT, GROUP, HD]),
                                        ALU.mult).then_inc(free, 1)
                        if og == GROUPS - 1:
                            released(("ot", og))
                            repeat_tail(on).then_inc(on_ready, 1)
                    if t % 16 == 10 and (attn if t < 48 else nxt):
                        g1, n1 = (t // 16 + 1) % GROUPS, (A if t < 48 else R)
                        ps, free = bank_of(("mx", g1))
                        k = GROUPS * n1 + g1 + 1
                        wait(dve, mx_in[g1], 16 * n1)
                        v.tensor_copy(mx_part[:, g1, 0, :], ps[0:16, 0:P]).then_inc(mxh_done, 1)
                        dve.wait_ge(mxh_done, k)
                        v.tensor_tensor(mx_rest[:, g1, :], ps[0:16, 0:P], mx_part[:, g1, 0, :], ALU.subtract).then_inc(free, 1)
                        released(("mx", g1))
                        v.tensor_copy(mx_part[:, g1, 1, :], mx_rest[:, g1, :]).then_inc(mxm_done, 1)
                        dve.wait_ge(mxm_done, k)
                        v.tensor_tensor(mx_part[:, g1, 2, :], mx_rest[:, g1, :], mx_part[:, g1, 1, :], ALU.subtract).then_inc(mxl_done, 1)
                    for f in range(3):
                        if prev and TRO_AT[f] + 1 == t:
                            ps, free = bank_of(("tro", f))
                            dve.wait_ge(tro_hi, 3 * Q + f + 1)
                            if f < 2:
                                low, high, whole = hpost[:, 2 + f, :], hpost[:, f, :], ps[:, :]
                            else:
                                low = high = hpost[TAIL:2 * TAIL, 4, :]
                                whole = ps[TAIL:2 * TAIL, :]
                            v.tensor_tensor(low, whole, high.bitcast(F32), ALU.subtract).then_inc(free, 1)
                    for tt in range(TT):
                        if nxt and V_AT[tt] + 1 == t:
                            ps, free = bank_of(("v", tt))
                            if tt == 0:
                                wait(dve, vcur_ready, A2)
                            v.tensor_copy(v_next[:, tt, 0:HEADS * VW].rearrange("p (h d) -> p h d", d=VW)[:, :, 0:HD],
                                          ps[:, 0:C].rearrange("p (h d) -> p h d", d=HD)).then_inc(free, 1)
                    for tt in range(TT):
                        if prev and PROJ_AT[tt] + 1 == t:
                            ps, free = bank_of(("proj", tt))
                            if tt == 0:
                                dve.wait_ge(gates_in, 16 * (Q + 1))
                            if tt < 2:
                                wait(dve, x2_done, TT * Q)
                            else:
                                dve.wait_ge(x1_done, TT * Q + tt - 1)
                            v.tensor_tensor(gated[:, tt % 2, :], ps[:, 0:C], gates[:, 0, :], ALU.mult).then_inc(free, 1)
                    for m in range(QK_TILES):
                        if nxt and QK_AT[m] + 1 == t:
                            ps, free = bank_of(("qk", m))
                            rows = QK_ROWS[m]
                            dve.wait_ge(qkh_done, QK_TILES * R + m + 1)
                            wait(dve, qkl_done, QK_TILES * R + m - 1)
                            v.tensor_tensor(rr[m % 2][0:rows, :], ps[0:rows, :], qk_part[0:rows, m % 2, 0, :],
                                            ALU.subtract).then_inc(free, 1)
                            released(("qk", m))
                            v.tensor_copy(qk_part[0:rows, m % 2, 1, :], rr[m % 2][0:rows, :]).then_inc(qkm_done, 1)
                    for part in range(3):
                        if prev and LN2_AT[part] == t:
                            norm(1, part)
                    if prev:
                        halves(1, t, [a + 1 for a in TRPOST_AT])
                    for h in range(2):
                        if prev and SPLIT_AT[h] == t:
                            if h == 0 and nxt:
                                released(("v", TT - 1))
                            for c in range(3):
                                high, low, part = split_hidden(h, c)
                                dve.wait_ge(gelu_done, 6 * Q + 3 * h + c + 1)
                                v.tensor_copy(high, part).then_inc(ghi_done, 1)
                                if c:
                                    dve.wait_ge(ghi_done, 6 * Q + 3 * h + c + 1)
                                    v.tensor_tensor(low, part, high.bitcast(F32), ALU.subtract).then_inc(glo_dve, 1)
                        for i in range(2):
                            if prev and FC2_AT[h][i][2] + 1 == t:
                                k = 2 * h + i
                                ps, free = bank_of(("fc2", k))
                                if k < 2:
                                    dve.wait_ge(x1_done, TT * (Q + 1))
                                else:
                                    dve.wait_ge(x2_done, TT * Q + k - 1)
                                v.tensor_tensor(gated[:, k % 2, :], ps[:, 0:C], gates[:, 1, :], ALU.mult).then_inc(free, 1)

            for layer in LAYERS:
                split_weights(layer)
                for name, attn, prev, nxt, first, times in PHASES:
                    if times == 1:
                        step(layer, name, attn, prev, nxt, BATCH * layer + first, 0)
                    else:
                        with dve.Fori(first, first + times) as b:
                            step(layer, name, attn, prev, nxt, b + BATCH * layer, b - first)

        @block.gpsimd
        def _(pool):
            g = nc.gpsimd
            pool.wait_ge(const_set, 1)

            def step(layer, name, attn, prev, nxt, n, turn):
                A, Q, R = counts(layer, name, n)

                def released(unit):
                    bank, before = banks.of(layer, name, unit, turn)
                    pool.wait_ge(lin_free[bank], before + 1)

                def inverse_root(kind):
                    pool.wait_ge(veps_done[kind], (R, Q)[kind] + 1)
                    g.tensor_tensor(rstd[:, kind, :], veps[:, kind, :], neghalf[:, :], ALU.pow).then_inc(rstd_done[kind], 1)

                def low_half(kind):
                    pool.wait_ge(hi_done[kind], 3 * (R, Q)[kind] + 1)
                    high, low = (hpre_main[:, 0, :], hpre_main[:, 2, :]) if kind == 0 else (hpost[:, 0, :], hpost[:, 2, :])
                    g.tensor_tensor(low, hf[0], high.bitcast(F32), ALU.subtract).then_inc(lo_pool[kind], 1)

                for t in range(NS):
                    if nxt and LN1_AT[1] == t:
                        inverse_root(0)
                    if nxt and TRPRE_AT[0] + 2 == t:
                        low_half(0)
                    for tt in range(TT):
                        if prev and PROJ_AT[tt] + 1 == t:
                            if tt == 0:
                                pool.wait_ge(xpost_in, 16 * (Q + 1))
                            released(("proj", tt))
                            g.tensor_tensor(x_post[:, tt, :], x_post[:, tt, :], gated[:, tt % 2, :], ALU.add).then_inc(x1_done, 1)
                    for m in range(QK_TILES):
                        if nxt and QK_AT[m] + 1 == t:
                            rows = QK_ROWS[m]
                            pool.wait_ge(qkm_done, QK_TILES * R + m + 1)
                            g.tensor_tensor(qk_part[0:rows, m % 2, 2, :], rr[m % 2][0:rows, :], qk_part[0:rows, m % 2, 1, :],
                                            ALU.subtract).then_inc(qkl_done, 1)
                    if prev and LN2_AT[1] == t:
                        inverse_root(1)
                    if prev and TRPOST_AT[0] + 2 == t:
                        low_half(1)
                    if prev and t == 30:
                        pool.wait_ge(norm_done[1], Q + 1)
                        pool.wait_ge(gates_in, 16 * (Q + 1))
                        g.tensor_tensor(x_post[:, :, :], x_post[:, :, :], gates[:, 2:3, :].to_broadcast([P, TT, C]),
                                        ALU.add).then_inc(gb_done, 1)
                    for h in range(2):
                        if prev and SPLIT_AT[h] == t:
                            pool.wait_ge(ghi_done, 6 * Q + 3 * h + 1)
                            part = uf[:, 0:3 * HALF].rearrange("p (f n) -> p f n", n=HALF)
                            g.tensor_tensor(hid[:, 1, 0:3, :], part, hid[:, 0, 0:3, :].bitcast(F32), ALU.subtract).then_inc(glo_pool, 1)
                        for i in range(2):
                            if prev and FC2_AT[h][i][2] + 1 == t:
                                k = 2 * h + i
                                released(("fc2", k))
                                pool.wait_ge(gb_done, Q + 1)
                                g.tensor_tensor(x_post[:, k, :], x_post[:, k, :], gated[:, k % 2, :], ALU.add).then_inc(x2_done, 1)

            for layer in LAYERS:
                for name, attn, prev, nxt, first, times in PHASES:
                    if times == 1:
                        step(layer, name, attn, prev, nxt, BATCH * layer + first, 0)
                    else:
                        with pool.Fori(first, first + times) as b:
                            step(layer, name, attn, prev, nxt, b + BATCH * layer, b - first)


_INS = ['x', 'cond_1152', 'L0_cond_W_qkv', 'L0_cond_b_qkv', 'L0_cond_W_proj', 'L0_cond_b_proj', 'L0_cond_W_fc1',
        'L0_cond_b_fc1', 'L0_cond_W_fc2', 'L0_cond_b_fc2', 'L0_cond_W_ada', 'L0_cond_b_ada', 'L1_cond_ln1_w',
        'L1_cond_ln1_b', 'L1_cond_wq', 'L1_cond_wk', 'L1_cond_wv', 'L1_cond_wo', 'L1_cond_wo_b', 'L1_cond_ln2_w',
        'L1_cond_ln2_b', 'L1_cond_fc1_w', 'L1_cond_fc1_b', 'L1_cond_fc2_w', 'L1_cond_fc2_b', 'L1_cond_ada_w',
        'L1_cond_ada_b']


def kernel(**inputs):
    import numpy as _np
    import concourse.bacc as _bacc
    from concourse import mybir as _mybir
    from concourse.bass_utils import run_bass_kernel_spmd as _run

    nc = _bacc.Bacc("TRN2", target_bir_lowering=False, num_devices=1)
    arrays, ap = {}, {}

    def give(name, a):
        arrays[name] = _np.ascontiguousarray(a)
        ap[name] = nc.dram_tensor(name, arrays[name].shape, _mybir.dt.from_np(arrays[name].dtype), kind="ExternalInput").ap()

    for name in _INS:
        give(name, inputs[name])
    give("ident_const", _np.eye(P, dtype=_np.float32))
    low_rows = _np.zeros((P, 1), _np.float32)
    low_rows[2 * TAIL:3 * TAIL] = -1.0
    low_rows[3 * TAIL + 1] = -1.0
    give("low_rows_const", low_rows)
    out = nc.dram_tensor("out_dram", (BATCH, TOK, C), _mybir.dt.float32, kind="ExternalOutput").ap()
    a, b = "L0_cond_", "L1_cond_"
    weights = (
        dict(qkv=[ap[a + "W_qkv"]], b_qkv=ap[a + "b_qkv"], proj=ap[a + "W_proj"], b_proj=ap[a + "b_proj"],
             fc1=ap[a + "W_fc1"], b_fc1=ap[a + "b_fc1"], fc2=ap[a + "W_fc2"], b_fc2=ap[a + "b_fc2"],
             ada=ap[a + "W_ada"], b_ada=ap[a + "b_ada"], ln=[]),
        dict(qkv=[ap[b + "wq"], ap[b + "wk"], ap[b + "wv"]], b_qkv=None, proj=ap[b + "wo"], b_proj=ap[b + "wo_b"],
             fc1=ap[b + "fc1_w"], b_fc1=ap[b + "fc1_b"], fc2=ap[b + "fc2_w"], b_fc2=ap[b + "fc2_b"],
             ada=ap[b + "ada_w"], b_ada=ap[b + "ada_b"],
             ln=[ap[b + n] for n in ("ln1_w", "ln1_b", "ln2_w", "ln2_b")]),
    )
    two_layer_block(nc, ap["x"], ap["cond_1152"], ap["low_rows_const"], ap["ident_const"], weights, out)
    r = _run(nc, [arrays], core_ids=[0])
    return r.results[0]["out_dram"]
```

```python
import numpy as np
import concourse.bass as bass
from concourse import mybir
from contextlib import ExitStack

F32 = mybir.dt.float32
F32R = mybir.dt.float32r
BF16 = mybir.dt.bfloat16
ALU = mybir.AluOpType
ACT = mybir.ActivationFunctionType
AX = mybir.AxisListType

BATCH, TOK, C = 8, 512, 288
HEADS = 16
HD = C // HEADS
FF = 4 * C
P = 128
TT = TOK // P
TAIL = C - 2 * P
CREP = 2 * P + 3 * TAIL
KT_TAIL = 3 * TAIL + 2
GROUP = 4
GROUPS = HEADS // GROUP
BLK = 7
QK_TILES = -(-2 * HEADS // BLK)
QK_ROWS = [min(BLK, 2 * HEADS - BLK * m) * HD for m in range(QK_TILES)]
PARTS = 3
Q_SLOTS = (0, 0, 1, 0, 2, 1)
K_SLOTS = (0, 1, 0, 2, 0, 1)
SLOTS = len(Q_SLOTS)
KS = SLOTS * HD
KM = KS + PARTS
VW = HD + 1
VPAD = (HEADS - 1) * VW + 32
FT = FF // P
HALF = TOK // 2
SCALE = float(HD) ** -0.5
EPS = (1e-6, 1e-5)
NS = GROUPS * TT * GROUP
AHEAD = 24
LD_STACK = 16 * 2 * SLOTS

STACK_AT = (28, 35, 50)
LN1_AT = (56, 57, 58, 60, 61, 62)
LN1_LOAD_AT = 46
TRPRE_AT = (0, 1, 2)
PRE_MOD_AT = (1, 2, 3)
PRE_HI_AT = (1, 2, 4)
PRE_LO_AT = (5, 5)
OT_AT = (4, 6, 7)
MX_AT = (9, 10, 11)
TRO_AT = (8, 8, 12)
TRO_HI_AT = (9, 9, 13)
TRO_LO_AT = (10, 10, 13)
PROJ_AT = (14, 15, 15, 16)
PROJ_OUT_AT = (15, 16, 16, 17)
QK_AT = (7, 12, 13, 20, 21)
QK_OUT_AT = (8, 13, 14, 21, 22)
QK_MID_AT = tuple(t + 1 for t in QK_OUT_AT)
V_AT = (23, 25, 31, 32)
V_OUT_AT = (24, 25, 32, 33)
LN2_AT = (18, 19, 20, 22, 23, 24)
TRPOST_AT = (26, 27, 28)
POST_MOD_AT = (27, 28, 29)
POST_HI_AT = (28, 29, 30)
POST_LO_AT = (30, 31)
FC1_AT = ((33, 34, 35, 36, 37), (39, 40, 40, 43, 45))
FC1_OUT_AT = ((34, 35, 36, 37, 38), (41, 42, 43, 44, 46))
GELU_AT = (38, 48)
SPLIT_AT = ((40, 41, 41), (52, 53, 54))
FC2_AT = (((47, 48, 48), (49, 50, 52)), ((55, 57, 58), (59, 60, 60)))
FC2_OUT_AT = (48, 52, 58, 61)
BIAS_AT = 33
VCUR_AT = 2
ADA_AT = tuple(range(30, 60, 3))
ADA_HEAD = 2
PAIRS = (FT + 1) // 2


def lin_units(attn, prev, nxt, ada):
    at = []
    for t in range(NS):
        for f in range(3):
            if nxt and TRPRE_AT[f] == t:
                at.append(("trpre", f))
        if t % 16 == OT_AT[1] and (prev if t < 16 else attn):
            at.append(("ot", (t // 16 - 1) % GROUPS))
        if t % 16 == MX_AT[0] and (attn if t < 48 else nxt):
            at.append(("mx", (t // 16 + 1) % GROUPS))
        for f in range(3):
            if prev and TRO_AT[f] == t:
                at.append(("tro", f))
        for n in range(TT):
            if nxt and V_AT[n] == t:
                at.append(("v", n))
        for n in range(TT):
            if prev and PROJ_AT[n] == t:
                at.append(("proj", n))
        for m in range(QK_TILES):
            if nxt and QK_AT[m] == t:
                at.append(("qk", m))
        for f in range(3):
            if prev and TRPOST_AT[f] == t:
                at.append(("trpost", f))
        for h in range(2):
            for u in range(PAIRS):
                if prev and FC1_AT[h][u] == t:
                    at.append(("fc1", PAIRS * h + u))
            for n in range(2):
                if prev and FC2_AT[h][n][0] == t:
                    at.append(("fc2", 2 * h + n))
        for n in range(len(ADA_AT)):
            if ada and ADA_AT[n] == t:
                at.append(("ada", ADA_HEAD + n))
    return at


class Phase:

    def __init__(self, name, first, times=1):
        self.name, self.first, self.times = name, first, times
        count = 2 * BATCH
        self.attn, self.prev = 0 <= first < count, 0 <= first - 1 < count
        self.nxt, self.norm = 0 <= first + 1 < count, 0 <= first + 2 < count
        self.prev_layer, self.next_layer, self.norm_layer = ((first + d) // BATCH for d in (-1, 1, 2))
        self.base = first // BATCH if times > 1 else 0
        self.ada = first == 0

    def counts(self, n):
        if isinstance(n, int):
            return max(n, 0), max(n - 1, 0), max(min(n + 1, 2 * BATCH), 0), min(n + 2, 2 * BATCH)
        return n, n - 1, n + 1, n + 2

    def batch(self, n, b, away, layer):
        return n + away - BATCH * layer if isinstance(n, int) else b + away


PHASES = (Phase("start", -2), Phase("pro", -1), Phase("first", 0), Phase("second", 1), Phase("mid0", 2, BATCH - 4),
          Phase("six", BATCH - 2), Phase("seven", BATCH - 1), Phase("eight", BATCH), Phase("nine", BATCH + 1),
          Phase("mid1", BATCH + 2, BATCH - 4), Phase("fourteen", 2 * BATCH - 2), Phase("last", 2 * BATCH - 1),
          Phase("epi", 2 * BATCH))

CH_QKV, CH_PROJ, CH_FC1, CH_FC2 = 9, 3, 12, FT
N_CHUNKS = CH_QKV + CH_PROJ + CH_FC1 + CH_FC2
AT_PROJ, AT_FC1, AT_FC2 = CH_QKV, CH_QKV + CH_PROJ, CH_QKV + CH_PROJ + CH_FC1
LOAD_LEAD = 3


def reload_table():
    early = AT_FC2 - AT_PROJ
    table = {"first": [(4 + 3 * i, AT_PROJ + i) for i in range(early)],
             "second": [(6 + 4 * i, AT_FC2 + i) for i in range(CH_FC2)],
             "six": [(31 + 3 * i, N_CHUNKS + i) for i in range(CH_QKV)]}
    fc1_at = [("eight", t) for t in (50, 52, 54, 56, 58, 60, 62)] + [("nine", t) for t in (9, 12, 14, 17, 19)]
    fc2_at = [("nine", t) for t in (22, 24, 27, 30, 32, 35, 37, 41, 45)]
    table["eight"] = [(t, N_CHUNKS + AT_PROJ + i) for i, t in enumerate((21, 25, 29))]
    table["nine"] = []
    for i, (step, t) in enumerate(fc1_at):
        table[step].append((t, N_CHUNKS + AT_FC1 + i))
    for i, (step, t) in enumerate(fc2_at):
        table[step].append((t, N_CHUNKS + AT_FC2 + i))
    return table


RELOAD = reload_table()


def is_tail(chunk):
    m = chunk % N_CHUNKS
    return (m < CH_QKV and m // 3 == 2) or m == AT_FC1 - 1 or AT_FC2 - 4 <= m < AT_FC2


def split_counts(chunks):
    tails = sum(is_tail(m) for m in range(chunks))
    return chunks - tails, tails


NLIN = 3


class Banks:

    def __init__(self):
        self.table, self.first = {}, {}
        used = [0] * NLIN
        for ph in PHASES:
            units = lin_units(ph.attn, ph.prev, ph.nxt, ph.ada)
            each = [sum(n % NLIN == b for n in range(len(units))) for b in range(NLIN)]
            for n, unit in enumerate(units):
                self.table[ph.name, unit] = (n % NLIN, used[n % NLIN] + n // NLIN, each[n % NLIN])
            self.first[ph.name] = (list(used), each)
            used = [u + ph.times * e for u, e in zip(used, each)]

    def of(self, ph, unit, turn):
        bank, before, each = self.table[ph.name, unit]
        return bank, before + turn * each

    def before(self, ph, bank, turn):
        used, each = self.first[ph.name]
        return used[bank] + turn * each[bank]


def two_layer_block(nc, x_in, cond, mask_in, ident_in, W, out):
    banks = Banks()
    x_mid = nc.dram_tensor("x_mid", (BATCH, TOK, C), F32).ap()
    qk_dram = nc.dram_tensor("qk_dram", (PARTS, 2 * HEADS, HD, TOK), BF16).ap()
    mx_dram = nc.dram_tensor("mx_dram", (GROUPS, PARTS, GROUP * TOK), BF16).ap()
    gate_dram = nc.dram_tensor("gate_dram", (2, BATCH, 3 * C), F32).ap()
    x_src = (x_in, x_mid)
    x_dst = (x_mid, out)

    ctx = ExitStack()
    with ctx:
        def sb(name, shape, dt=F32):
            return ctx.enter_context(nc.sbuf_tensor(name, list(shape), dt))

        def sem(name):
            return ctx.enter_context(nc.semaphore(name))

        w_qkv = sb("w_qkv", (P, 5, 3 * C), F32R)
        w_proj = sb("w_proj", (P, 5, C), F32R)
        w_fc1 = sb("w_fc1", (P, 5, FF), F32R)
        w_fc2 = sb("w_fc2", (P, 2, FT, C), F32R)
        q_stack = sb("q_stack", (P, GROUPS, GROUP, TOK), BF16)
        k_stack = sb("k_stack", (P, GROUPS, GROUP, TOK), BF16)
        v_next = sb("v_next", (P, TT, VPAD))
        v_cur = sb("v_cur", (P, TT, VPAD))
        probs = sb("probs", (P, 2, GROUP, TOK))
        hid = sb("hid", (P, 2, FT, HALF), F32R)
        hpre_main = hid[:, :, :, :].rearrange("p a f n -> p (a f n)")[:, 0:4 * TOK]\
            .rearrange("p (a n) -> p a n", a=4)
        hpre_tail = sb("hpre_tail", (P, TOK), F32R)
        hpost = sb("hpost", (P, 5, TOK), F32R)
        uf = sb("uf", (P, FT * HALF))
        hf = [uf[:, TOK * n:TOK * (n + 1)] for n in range(3)]
        rr_own = sb("rr_own", (P, TOK))
        rr = [uf[:, 3 * TOK:4 * TOK], rr_own[:, :]]
        ada_buf = [uf[:, FF * n:FF * n + 3 * C].rearrange("p (k n) -> p k n", k=3) for n in range(2)]
        w_stage = sb("w_stage", (P, 2, C))
        w_first = probs[:, :, :, :].rearrange("p a h n -> p (a h n)")

        def stage(chunk):
            return w_first[:, C * chunk:C * (chunk + 1)] if chunk < CH_QKV else w_stage[:, chunk % 2, :]
        qk_part = sb("qk_part", (P, 2, PARTS, TOK), BF16)
        x_pre = sb("x_pre", (P, TT, C))
        x_post = sb("x_post", (P, TT, C))
        xn = sb("xn", (P, TT, CREP))
        on = sb("on", (P, TT, CREP))
        o_sb = sb("o_sb", (P, TOK))
        gates = sb("gates", (P, 3, C))
        gated = sb("gated", (P, 2, C))
        mx = sb("mx", (P, GROUPS, 16))
        mx_part = sb("mx_part", (16, GROUPS, PARTS, P), BF16)
        mx_rest = sb("mx_rest", (16, GROUPS, P))
        osum = sb("osum", (P, TT, GROUP, 1))
        stats = sb("stats", (P, 2, TT, 6))
        mv = sb("mv", (P, 2, TT, 2))
        veps = sb("veps", (P, 2, TT))
        rstd = sb("rstd", (P, 2, TT))
        neghalf = sb("neghalf", (P, TT))
        ident = sb("ident", (P, P))
        lomask = sb("lomask", (P, 1))
        mod_a = sb("mod_a", (P, 2, 2, 3, BATCH))
        mod_b = sb("mod_b", (P, 2, 2, 3, BATCH))
        csil = x_post[0:BATCH, :, :]
        csil_t = sb("csil_t", (P, 3, BATCH))
        prm = [o_sb[0:6, 0:C], gated[0:10, 0, :]]
        prm_t = sb("prm_t", (P, 2, 3, 10))
        gate_sb = x_post[0:BATCH, 0:3, :]
        gate_bias = gates[0:BATCH, :, :]

        s1_ps = [ctx.enter_context(nc.psum_tensor(f"s1_ps{n}", [P, TOK], F32)) for n in range(2)]
        s2_ps = [ctx.enter_context(nc.psum_tensor(f"s2_ps{n}", [P, TOK], F32)) for n in range(2)]
        pv_ps = ctx.enter_context(nc.psum_tensor("pv_ps", [P, TOK], F32))
        lin_ps = [ctx.enter_context(nc.psum_tensor(f"lin_ps{n}", [P, TOK], F32)) for n in range(NLIN)]

        def per_kind(name):
            return [sem(name + "_pre"), sem(name + "_post")]

        lin_done = [sem(f"lin_done{n}") for n in range(NLIN)]
        lin_free = [sem(f"lin_free{n}") for n in range(NLIN)]
        stack_in = [sem(f"stack_in{g}") for g in range(GROUPS)]
        s1_done, mx_done = sem("s1_done"), sem("mx_done")
        mxh_done, mxm_done, mxl_done = sem("mxh_done"), sem("mxm_done"), sem("mxl_done")
        mx_out = [sem(f"mx_out{g}") for g in range(GROUPS)]
        mx_in = [sem(f"mx_in{g}") for g in range(GROUPS)]
        s2_done, exp_done = sem("s2_done"), sem("exp_done")
        pv_done, o_evac = sem("pv_done"), sem("o_evac")
        osum_done, on_ready = sem("osum_done"), sem("on_ready")
        vcur_ready = sem("vcur_ready")
        xpre_in = sem("xpre_in")
        qk_out = [sem(f"qk_out{n}") for n in range(2)]
        qkh_done, qkm_done, qkl_done = sem("qkh_done"), sem("qkm_done"), sem("qkl_done")
        stat_done, mv_done = per_kind("stat_done"), per_kind("mv_done")
        veps_done, rstd_done = per_kind("veps_done"), per_kind("rstd_done")
        norm_done, xn_ready = per_kind("norm_done"), per_kind("xn_ready")
        hi_done = per_kind("hi_done")
        lo_dve, lo_pool = per_kind("lo_dve"), per_kind("lo_pool")
        xpost_in, gates_in = sem("xpost_in"), sem("gates_in")
        tro_hi = sem("tro_hi")
        x1_done, gb_done, x2_done = sem("x1_done"), sem("gb_done"), sem("x2_done")
        gelu_done, ghi_done, glo_dve, glo_pool = sem("gelu_done"), sem("ghi_done"), sem("glo_dve"), sem("glo_pool")
        stored = sem("stored")
        const_in, const_set, cond_in, ones_set = sem("const_in"), sem("const_set"), sem("cond_in"), sem("ones_set")
        cond_exp, cond_step, cond_tr = sem("cond_exp"), sem("cond_step"), sem("cond_tr")
        prm_in = [sem(f"prm_in{n}") for n in range(2)]
        prm_tr, prm_done = sem("prm_tr"), sem("prm_done")
        ada_in = [sem(f"ada_in{n}") for n in range(2)]
        ada_bias_in, ada_mm, ada_vec = sem("ada_bias_in"), sem("ada_mm"), sem("ada_vec")
        gate_step, gate_out, mod_step = sem("gate_step"), sem("gate_out"), sem("mod_step")
        w_in = [sem(f"w_in{n}") for n in range(2)]
        w_first_in = sem("w_first_in")
        w_high = sem("w_high")
        w_low, w_tail = sem("w_low"), sem("w_tail")

        def wait(eng, s, value):
            if not isinstance(value, int) or value > 0:
                eng.wait_ge(s, value)

        LAYERS = range(2)

        def weight_chunk(chunk):
            layer, m = divmod(chunk, N_CHUNKS)
            w = W[layer]
            if m >= AT_FC2:
                f = m - AT_FC2
                return "f", w_fc2, f, slice(0, C), w["fc2"][P * f:P * (f + 1), :], None
            if m >= AT_FC1:
                k, i = divmod(m - AT_FC1, 4)
                dst, src, bias = w_fc1, w["fc1"], w["b_fc1"]
            elif m >= AT_PROJ:
                k, i, dst, src, bias = m - AT_PROJ, 0, w_proj, w["proj"], w["b_proj"]
            else:
                k, i = divmod(m, 3)
                dst, src, bias = w_qkv, w["qkv"][i if len(w["qkv"]) > 1 else 0], w["b_qkv"]
            cols = slice(C * i, C * (i + 1))
            src_cols = cols if src.shape[1] > C else slice(0, C)
            rows = slice(P * k, P * (k + 1)) if k < 2 else slice(2 * P, C)
            return "k", dst, k, cols, src[rows, src_cols], bias[cols] if bias is not None and k == 2 else None

        def chunk_dmas(chunk):
            return (3 + 2 * (weight_chunk(chunk)[5] is not None)) if is_tail(chunk) else 1

        def chunk_in(chunk):
            if chunk < CH_QKV:
                return 16 * sum(chunk_dmas(m) for m in range(CH_QKV))
            return 16 * sum(chunk_dmas(m) for m in range(CH_QKV, chunk + 1) if (chunk - m) % 2 == 0)

        block = ctx.enter_context(nc.Block())

        @block.sync
        def _(sp):
            sp.dma_start(ident[:, :], ident_in).then_inc(const_in, 16)
            sp.dma_start(lomask[:, :], mask_in).then_inc(const_in, 16)
            sp.dma_start(csil[:, 0, :], cond).then_inc(cond_in, 16)

            def load_ada(n):
                if n >= ADA_HEAD + 2:
                    bank, before = banks.of(PHASES[2], ("ada", n - 2), 0)
                    sp.wait_ge(lin_done[bank], before + 1)
                elif n >= 2:
                    sp.wait_ge(ada_mm, n - 1)
                src, cols = W[n // 6]["ada"], slice(C * (n % 6), C * (n % 6) + C)
                sp.dma_start(ada_buf[n % 2][:, 0:2, :], src[0:2 * P, cols].rearrange("(k p) n -> p k n", p=P)).then_inc(ada_in[n % 2], 16)
                sp.dma_start(ada_buf[n % 2][0:TAIL, 2, :], src[2 * P:C, cols]).then_inc(ada_in[n % 2], 16)

            def load_prm(layer):
                w = W[layer]
                sp.dma_start(prm[layer][0:6, :], w["b_ada"].rearrange("(r n) -> r n", n=C)).then_inc(prm_in[layer], 16)
                for r, v in enumerate(w["ln"]):
                    sp.dma_start(prm[layer][6 + r:7 + r, :], v.rearrange("(o n) -> o n", o=1)).then_inc(prm_in[layer], 16)

            load_prm(0)
            for n in range(ADA_HEAD):
                load_ada(n)

            def load_gate_bias(layer):
                w = W[layer]
                for r, v in enumerate((w["b_ada"][2 * C:3 * C], w["b_ada"][5 * C:6 * C], w["b_fc2"])):
                    sp.dma_start(gate_bias[:, r, :], v.rearrange("(o n) -> o n", o=1).to_broadcast([BATCH, C])
                                 ).then_inc(ada_bias_in, 16)

            def load_chunk(chunk):
                _, _, _, _, src, bias = weight_chunk(chunk)
                buf, s = stage(chunk), w_in[chunk % 2] if chunk >= CH_QKV else w_first_in
                if chunk >= CH_QKV + 2:
                    low, tail = split_counts(chunk - 1)
                    wait(sp, w_low, low)
                    wait(sp, w_tail, tail)
                if not is_tail(chunk):
                    sp.dma_start(buf, src).then_inc(s, 16)
                    return
                for r in range(3):
                    sp.dma_start(buf[TAIL * r:TAIL * (r + 1), :], src).then_inc(s, 16)
                if bias is not None:
                    for r in range(2):
                        sp.dma_start(buf[3 * TAIL + r:3 * TAIL + r + 1, :], bias.rearrange("(o n) -> o n", o=1)).then_inc(s, 16)

            def load_stack(g, n):
                if isinstance(n, int) and n == 0:
                    sp.wait_ge(ones_set, 1)
                wait(sp, s2_done, NS * (n - 1) + 16 * (g + 1))
                for stack, first, slots in ((q_stack, 0, Q_SLOTS), (k_stack, HEADS, K_SLOTS)):
                    for r, part in enumerate(slots):
                        heads = qk_dram[part, first + GROUP * g:first + GROUP * (g + 1), :, :]
                        sp.dma_start(stack[HD * r:HD * (r + 1), g, :, :], heads.rearrange("h d n -> d h n")).then_inc(stack_in[g], 16)

            def step(ph, n, b, turn):
                attn, prev, nxt = ph.attn, ph.prev, ph.nxt
                A, Q, R, L = ph.counts(n)
                def apart():
                    sp.wait_ge(const_in, 32)

                for t in range(NS):
                    if t == LN1_LOAD_AT and ph.norm:
                        apart()
                        wait(sp, norm_done[0], L)
                        x_next = x_src[ph.norm_layer][ph.batch(n, b, 2, ph.norm_layer), :, :]
                        sp.dma_start(x_pre[:, :, :], x_next.rearrange("(t p) n -> p t n", p=P)).then_inc(xpre_in, 16)
                    if t == 0 and prev:
                        apart()
                        wait(sp, stored, 16 * TT * Q)
                        at = ph.batch(n, b, -1, ph.prev_layer)
                        sp.dma_start(x_post[:, :, :], x_src[ph.prev_layer][at, :, :].rearrange("(t p) n -> p t n", p=P)).then_inc(xpost_in, 16)
                        sp.dma_start(gates[:, :, :].rearrange("p a n -> p (a n)"),
                                     gate_dram[ph.prev_layer, at, :].rearrange("(o n) -> o n", o=1).to_broadcast([P, 3 * C])).then_inc(gates_in, 16)
                    for at, chunk in RELOAD.get(ph.name, ()):
                        if max(at - LOAD_LEAD, 0) == t:
                            load_chunk(chunk)
                    if ph.ada and t + 4 in ADA_AT:
                        if t + 4 == ADA_AT[0]:
                            sp.wait_ge(lo_pool[0], R + 1)
                            sp.wait_ge(lo_dve[0], 2 * (R + 1))
                            sp.wait_ge(qkl_done, QK_TILES * (R + 1))
                        load_ada(ADA_HEAD + ADA_AT.index(t + 4))
                    for layer in LAYERS:
                        if ph.ada and t == ADA_AT[6 * layer + 5 - ADA_HEAD] + 3:
                            sp.wait_ge(gate_step, layer + 1)
                            sp.dma_start(gate_dram[layer, :, :], gate_sb[:, :, :].rearrange("p a n -> p (a n)")).then_inc(gate_out, 16)
                            if layer == 0:
                                load_gate_bias(1)
                            else:
                                sp.wait_ge(gate_out, 32)
                    if t == 0 and attn:
                        load_stack(GROUPS - 1, A)
                    if t % 16 == MX_AT[2] and (attn if t < 48 else nxt):
                        g, m = (t // 16 + 1) % GROUPS, (A if t < 48 else R)
                        sp.wait_ge(mxl_done, GROUPS * m + g + 1)
                        sp.dma_start(mx_dram[g, :, :].rearrange("a (r n) -> r a n", n=P), mx_part[:, g, :, :]).then_inc(mx_out[g], 16)
                        sp.wait_ge(mx_out[g], 16 * (m + 1))
                        sp.dma_start(q_stack[KS:KM, g, :, :], mx_dram[g, :, :].rearrange("a (h n) -> a h n", n=TOK)).then_inc(mx_in[g], 16)
                    for m in range(QK_TILES):
                        if nxt and QK_MID_AT[m] + 1 == t:
                            rows = QK_ROWS[m]
                            if m == 0:
                                for g in range(GROUPS):
                                    wait(sp, stack_in[g], LD_STACK * R)
                            sp.wait_ge(qkl_done, QK_TILES * R + m + 1)
                            if m == QK_TILES - 1:
                                sp.wait_ge(qk_out[1], 96 * (R + 1))
                            for part in range(PARTS):
                                sp.dma_start(qk_dram[part, BLK * m:BLK * m + rows // HD, :, :].rearrange("h d n -> (h d) n"),
                                             qk_part[0:rows, m % 2, part, :]).then_inc(qk_out[m % 2], 16)
                    if t in STACK_AT and nxt:
                        if t == STACK_AT[0]:
                            sp.wait_ge(qk_out[0], 144 * (R + 1))
                        load_stack(STACK_AT.index(t), R)
                    for h in range(2):
                        for i in range(2):
                            if prev and FC2_OUT_AT[2 * h + i] == t:
                                tt = 2 * h + i
                                apart()
                                sp.wait_ge(x2_done, TT * Q + tt + 1)
                                sp.dma_start(x_dst[ph.prev_layer][ph.batch(n, b, -1, ph.prev_layer), tt * P:(tt + 1) * P, :], x_post[:, tt, :]).then_inc(stored, 16)

            for ph in PHASES:
                if ph.times == 1:
                    step(ph, ph.first, None, 0)
                else:
                    first = ph.first - BATCH * ph.base
                    with sp.Fori(first, first + ph.times) as b:
                        step(ph, b + BATCH * ph.base, b, b - first)
                if ph.name == "start":
                    for chunk in range(CH_QKV):
                        load_chunk(chunk)
                    load_prm(1)
                    load_gate_bias(0)
            sp.wait_ge(stored, 16 * TT * 2 * BATCH)

        @block.tensor
        def _(pe):
            mm, tr = nc.tensor.matmul, nc.tensor.transpose
            pe.wait_ge(const_in, 32)
            pe.wait_ge(cond_step, 3)
            for k in range(3):
                rows = P if k < 2 else TAIL
                last = tr(lin_ps[0][0:rows, BATCH * k:BATCH * (k + 1)], csil[:, 3, P * k:P * k + rows], ident[0:BATCH, 0:BATCH])
            last.then_inc(cond_tr, 1)
            pe.wait_ge(cond_step, 4)
            def transpose_prm(layer):
                rows = (6, 10)[layer]
                pe.wait_ge(prm_in[layer], (16, 16 * 5)[layer])
                for k in range(5):
                    cols, c0, p0 = (P, P * k, 0) if k < 2 else (TAIL, 2 * P, TAIL * (k - 2))
                    last = mm(lin_ps[1 - layer][p0:p0 + cols, 16 * min(k, 2):16 * min(k, 2) + rows], prm[layer][:, c0:c0 + cols],
                              ident[0:rows, 0:rows], start=True, stop=True)
                last.then_inc(prm_tr, 1)

            transpose_prm(0)

            def ada_products(n, ps):
                pe.wait_ge(ada_in[n % 2], 32 * (n // 2 + 1))
                buf = ada_buf[n % 2]
                if n % 3 == 2:
                    for k in range(3):
                        rows = P if k < 2 else TAIL
                        last = mm(ps[0:BATCH, 0:C], csil_t[0:rows, k, :], buf[0:rows, k, :], start=(k == 0), stop=(k == 2))
                    return last
                for f in range(5):
                    cols = P if f < 2 else TAIL
                    p0 = 0 if f < 2 else TAIL * (f - 2)
                    c0 = P * min(f, 2)
                    for k in range(3):
                        rows = P if k < 2 else TAIL
                        last = mm(ps[p0:p0 + cols, BATCH * min(f, 2):BATCH * (min(f, 2) + 1)],
                                  buf[0:rows, k, c0:c0 + cols], csil_t[0:rows, k, :], start=(k == 0), stop=(k == 2))
                return last

            for n in range(ADA_HEAD):
                if n:
                    pe.wait_ge(ada_vec, n)
                ada_products(n, lin_ps[2]).then_inc(ada_mm, 1)
            transpose_prm(1)

            def split_products(ps, acts, weights, tail_act, tail_weight):
                pairs = [(0, 0), (1, 1), (2, 0), (3, 1), (0, 2), (1, 3)]
                for i, (a, w) in enumerate(pairs):
                    lhs, rhs = (acts(a), weights(w))
                    mm(ps, lhs, rhs, start=(i == 0), stop=False)
                return mm(ps, tail_act, tail_weight, start=False, stop=True)

            def hp(kind, tile):
                if kind == 0:
                    return hpre_main[:, tile, :] if tile < 4 else hpre_tail[0:KT_TAIL, :]
                return hpost[:, tile, :] if tile < 4 else hpost[0:KT_TAIL, 4, :]

            pe.wait_ge(prm_done, 2)
            pe.wait_ge(ones_set, 1)
            pe.wait_ge(ada_vec, ADA_HEAD)

            def step(ph, n, b, turn):
                attn, prev, nxt = ph.attn, ph.prev, ph.nxt
                A, Q, R, L = ph.counts(n)

                def weights_ready(step, chunks):
                    if ph.name in step:
                        low, tail = split_counts(chunks + N_CHUNKS * step.index(ph.name))
                        pe.wait_ge(w_low, low)
                        pe.wait_ge(w_tail, tail)

                def bank_of(unit):
                    bank, before = banks.of(ph, unit, turn)
                    wait(pe, lin_free[bank], before)
                    return lin_ps[bank], lin_done[bank]

                def pre_ready():
                    pe.wait_ge(lo_pool[0], R + 1)
                    pe.wait_ge(lo_dve[0], 2 * (R + 1))
                    weights_ready(("pro", "seven"), CH_QKV)

                def transposes(kind, f):
                    ps, done = bank_of((("trpre", "trpost")[kind], f))
                    pe.wait_ge(xn_ready[kind], ((R, Q)[kind]) + 1)
                    cols = P if f < 2 else 3 * TAIL
                    for tt in range(TT):
                        last = tr(ps[0:cols, P * tt:P * (tt + 1)], xn[:, tt, P * f:P * f + cols], ident[:, :])
                    last.then_inc(done, 1)

                for t in range(NS):
                    g, kt, j = t // 16, (t // 4) % TT, t % 4
                    if attn:
                        if kt == 0 and j == 0:
                            pe.wait_ge(mx_in[g], 16 * (A + 1))
                        wait(pe, exp_done, NS * A + t - 1)
                        mm(s2_ps[t % 2][:, :], k_stack[0:KM, g, j, P * kt:P * (kt + 1)], q_stack[0:KM, g, j, :],
                           start=True, stop=True).then_inc(s2_done, 1)
                    s = t + AHEAD
                    if attn if s < NS else nxt:
                        g1, l1, n1 = (s // 16) % GROUPS, s % 16, (A if s < NS else R)
                        if l1 == 0:
                            pe.wait_ge(stack_in[g1], LD_STACK * (n1 + 1))
                        wait(pe, mx_done, NS * n1 + s % NS - 1)
                        qt = l1 % TT
                        mm(s1_ps[s % 2][:, :], q_stack[0:KS, g1, l1 // TT, P * qt:P * (qt + 1)], k_stack[0:KS, g1, l1 // TT, :],
                           start=True, stop=True).then_inc(s1_done, 1)
                    if t % 4 == 2 and (attn if t >= 4 else prev):
                        slot, n1 = (t // 4 - 1) % 16, A - (t < 4)
                        pg, pkt = slot // TT, slot % TT
                        pe.wait_ge(exp_done, NS * n1 + 4 * (slot + 1))
                        if pkt == 0:
                            wait(pe, o_evac, GROUPS * n1 + pg)
                        if slot == 0:
                            pe.wait_ge(vcur_ready, n1 + 1)
                        for h in range(GROUP):
                            c0 = VW * (GROUP * pg + h)
                            last = mm(pv_ps[32 * h:32 * (h + 1), :], v_cur[:, pkt, c0:c0 + 32], probs[:, slot % 2, h, :],
                                      start=(pkt == 0), stop=(pkt == TT - 1))
                        last.then_inc(pv_done, 1)
                    for f in range(3):
                        if nxt and TRPRE_AT[f] == t:
                            transposes(0, f)
                    if t % 16 == OT_AT[1] and (prev if t < 16 else attn):
                        og, n1 = (t // 16 - 1) % GROUPS, A - (t < 16)
                        ps, done = bank_of(("ot", og))
                        pe.wait_ge(o_evac, GROUPS * n1 + og + 1)
                        for tt in range(TT):
                            last = tr(ps[:, P * tt:P * (tt + 1)], o_sb[:, P * tt:P * (tt + 1)], ident[:, :])
                        last.then_inc(done, 1)
                    if t % 16 == MX_AT[0] and (attn if t < 48 else nxt):
                        g1, n1 = (t // 16 + 1) % GROUPS, (A if t < 48 else R)
                        ps, done = bank_of(("mx", g1))
                        pe.wait_ge(mx_done, NS * n1 + 16 * (g1 + 1))
                        tr(ps[0:16, 0:P], mx[:, g1, :], ident[:, :]).then_inc(done, 1)
                    for f in range(3):
                        if prev and TRO_AT[f] == t:
                            ps, done = bank_of(("tro", f))
                            pe.wait_ge(on_ready, Q + 1)
                            cols = P if f < 2 else 3 * TAIL
                            for tt in range(TT):
                                last = tr(ps[0:cols, P * tt:P * (tt + 1)], on[:, tt, P * f:P * f + cols], ident[:, :])
                            last.then_inc(done, 1)
                    for tt in range(TT):
                        if nxt and V_AT[tt] == t:
                            ps, done = bank_of(("v", tt))
                            pre_ready()
                            tok = slice(P * tt, P * (tt + 1))
                            split_products(ps[:, 0:C], lambda a: hp(0, a)[:, tok], lambda w: w_qkv[:, w, 2 * C:3 * C],
                                           hp(0, 4)[:, tok], w_qkv[0:KT_TAIL, 4, 2 * C:3 * C]).then_inc(done, 1)
                    for tt in range(TT):
                        if prev and PROJ_AT[tt] == t:
                            ps, done = bank_of(("proj", tt))
                            landed = {}
                            for f in range(3):
                                tro_bank, before = banks.of(ph, ("tro", f), turn)
                                landed[tro_bank] = before + 1
                            for tro_bank, count in landed.items():
                                pe.wait_ge(lin_free[tro_bank], count)
                            weights_ready(("second", "nine"), AT_FC1)
                            tok = slice(P * tt, P * (tt + 1))
                            split_products(ps[:, 0:C], lambda a: hp(1, a)[:, tok], lambda w: w_proj[:, w, :],
                                           hp(1, 4)[:, tok], w_proj[0:KT_TAIL, 4, :]).then_inc(done, 1)
                    for m in range(QK_TILES):
                        if nxt and QK_AT[m] == t:
                            ps, done = bank_of(("qk", m))
                            pre_ready()
                            rows = QK_ROWS[m]
                            cols = slice(BLK * HD * m, BLK * HD * m + rows)
                            pairs = [(0, 0), (1, 1), (2, 0), (3, 1), (0, 2), (1, 3)]
                            for i, (a, w) in enumerate(pairs):
                                mm(ps[0:rows, :], w_qkv[:, w, cols], hp(0, a), start=(i == 0), stop=False)
                            mm(ps[0:rows, :], w_qkv[0:KT_TAIL, 4, cols], hp(0, 4), start=False, stop=True).then_inc(done, 1)
                    for f in range(3):
                        if prev and TRPOST_AT[f] == t:
                            transposes(1, f)
                    for h in range(2):
                        tok = slice(HALF * h, HALF * (h + 1))
                        for u in range(PAIRS):
                            if prev and FC1_AT[h][u] == t:
                                ps, done = bank_of(("fc1", PAIRS * h + u))
                                pe.wait_ge(lo_pool[1], Q + 1)
                                pe.wait_ge(lo_dve[1], 2 * (Q + 1))
                                weights_ready(("second", "nine"), AT_FC2)
                                for f in range(2 * u, min(2 * u + 2, FT)):
                                    o = ps[:, HALF * (f % 2):HALF * (f % 2 + 1)]
                                    pairs = [(0, 0), (1, 1), (2, 0), (3, 1), (0, 2), (1, 3)]
                                    for i, (a, w) in enumerate(pairs):
                                        mm(o, w_fc1[:, w, P * f:P * (f + 1)], hp(1, a)[:, tok], start=(i == 0), stop=False)
                                    last = mm(o, w_fc1[0:KT_TAIL, 4, P * f:P * (f + 1)], hp(1, 4)[:, tok], start=False, stop=True)
                                last.then_inc(done, 1)
                        for i in range(2):
                            for c in range(3):
                                if prev and FC2_AT[h][i][c] == t:
                                    if c == 0:
                                        fc2_ps, fc2_bank = bank_of(("fc2", 2 * h + i))
                                        weights_ready(("second", "nine"), N_CHUNKS)
                                    pe.wait_ge(ghi_done, 6 * Q + 3 * h + c + 1)
                                    if c == 2:
                                        pe.wait_ge(glo_pool, 2 * Q + h + 1)
                                    else:
                                        pe.wait_ge(glo_dve, 4 * Q + 2 * h + c + 1)
                                    for f in range(3 * c, 3 * c + 3):
                                        for a, w in ((0, 0), (1, 0), (0, 1)):
                                            last = mm(fc2_ps[:, 0:C], hid[:, a, f, P * i:P * (i + 1)], w_fc2[:, w, f, :],
                                                      start=(f == 0 and a == 0 and w == 0), stop=(f == FT - 1 and w == 1))
                                    if c == 2:
                                        last.then_inc(fc2_bank, 1)
                    if ph.ada and t in ADA_AT:
                        ada_n = ADA_HEAD + ADA_AT.index(t)
                        ps, done = bank_of(("ada", ada_n))
                        ada_products(ada_n, ps).then_inc(done, 1)

            for ph in PHASES:
                if ph.times == 1:
                    step(ph, ph.first, None, 0)
                else:
                    first = ph.first - BATCH * ph.base
                    with pe.Fori(first, first + ph.times) as b:
                        step(ph, b + BATCH * ph.base, b, b - first)

        @block.scalar
        def _(act):
            fn = nc.scalar.activation
            gelu = (ACT.Gelu_apprx_tanh, ACT.Gelu)
            act.wait_ge(cond_in, 16)
            fn(csil[:, 1, :], csil[:, 0, :], ACT.Exp, scale=-1.0).then_inc(cond_exp, 1)
            act.wait_ge(ada_vec, ADA_HEAD)

            def step(ph, n, b, turn):
                attn, prev, nxt = ph.attn, ph.prev, ph.nxt
                A, Q, R, L = ph.counts(n)
                R2 = R + 1 if nxt else R

                def bank_of(unit):
                    bank, before = banks.of(ph, unit, turn)
                    act.wait_ge(lin_done[bank], before + 1)
                    return lin_ps[bank], lin_free[bank]

                def modulate(kind, f):
                    ps, free = bank_of((("trpre", "trpost")[kind], f))
                    rows = P if f < 2 else 3 * TAIL
                    layer = (ph.next_layer, ph.prev_layer)[kind]
                    bb = ph.batch(n, b, (1, -1)[kind], layer)
                    fn(hf[f][0:rows, :], ps[0:rows, :], ACT.Identity, scale=mod_a[0:rows, layer, kind, f, bass.ds(bb, 1)],
                       bias=mod_b[0:rows, layer, kind, f, bass.ds(bb, 1)]).then_inc(free, 1)

                if ph.name == "second":
                    act.wait_ge(mod_step, 4)
                    act.wait_ge(gate_step, 2)
                for t in range(NS):
                    if attn:
                        slot = t // 4
                        act.wait_ge(s2_done, NS * A + t + 1)
                        if t % 4 == 0:
                            wait(act, pv_done, 16 * A + slot - 1)
                        fn(probs[:, slot % 2, t % 4, :], s2_ps[t % 2][:, :], ACT.Exp, scale=SCALE).then_inc(exp_done, 1)
                    if t % 16 == OT_AT[0] and (prev if t < 16 else attn):
                        og, n1 = (t // 16 - 1) % GROUPS, A - (t < 16)
                        act.wait_ge(pv_done, 16 * n1 + TT * (og + 1))
                        wait(act, osum_done, GROUPS * n1 + og)
                        fn(o_sb[:, :], pv_ps[:, :], ACT.Copy).then_inc(o_evac, 1)
                    for f in range(3):
                        if nxt and PRE_MOD_AT[f] == t:
                            if f == 0:
                                wait(act, glo_dve, 4 * Q)
                                wait(act, glo_pool, 2 * Q)
                                wait(act, qkl_done, QK_TILES * R)
                            modulate(0, f)
                    for f in range(3):
                        if prev and TRO_HI_AT[f] == t:
                            ps, _ = bank_of(("tro", f))
                            rows = P if f < 2 else 3 * TAIL
                            fn(hpost[0:rows, f if f < 2 else 4, :], ps[0:rows, :], ACT.Copy).then_inc(tro_hi, 1)
                    for m in range(QK_TILES):
                        if nxt and QK_OUT_AT[m] == t:
                            ps, _ = bank_of(("qk", m))
                            rows = QK_ROWS[m]
                            wait(act, qk_out[m % 2], (144, 96)[m % 2] * R + 48 * (m // 2))
                            fn(qk_part[0:rows, m % 2, 0, :], ps[0:rows, :], ACT.Copy).then_inc(qkh_done, 1)
                    for m in range(QK_TILES):
                        if nxt and QK_MID_AT[m] == t:
                            rows = QK_ROWS[m]
                            qk_bank, before = banks.of(ph, ("qk", m), turn)
                            act.wait_ge(lin_free[qk_bank], before + 1)
                            fn(qk_part[0:rows, m % 2, 1, :], rr[m % 2][0:rows, :], ACT.Copy).then_inc(qkm_done, 1)
                    for tt in range(TT):
                        if nxt and V_OUT_AT[tt] == t:
                            ps, free = bank_of(("v", tt))
                            if tt == 0:
                                wait(act, vcur_ready, A + 1 if attn else A)
                            fn(v_next[:, tt, 0:HEADS * VW].rearrange("p (h d) -> p h d", d=VW)[:, :, 0:HD],
                               ps[:, 0:C].rearrange("p (h d) -> p h d", d=HD), ACT.Copy).then_inc(free, 1)
                    for f in range(3):
                        if prev and POST_MOD_AT[f] == t:
                            if f == 0:
                                wait(act, lo_pool[0], R2)
                                wait(act, lo_dve[0], 2 * R2)
                            modulate(1, f)
                    for h in range(2):
                        for u in range(PAIRS):
                            if prev and FC1_OUT_AT[h][u] == t:
                                ps, free = bank_of(("fc1", PAIRS * h + u))
                                if h == 1 and u < 2:
                                    act.wait_ge(glo_dve, 4 * Q + u + 1)
                                if h == 1 and u == 3:
                                    act.wait_ge(glo_pool, 2 * Q + 1)
                                if u == 0 and h == 0:
                                    act.wait_ge(lo_dve[1], 2 * (Q + 1))
                                    act.wait_ge(lo_pool[1], Q + 1)
                                    wait(act, qkl_done, QK_TILES * R2)
                                size = HALF * (min(2 * u + 2, FT) - 2 * u)
                                fn(uf[:, TOK * u:TOK * u + size], ps[:, 0:size], ACT.Copy).then_inc(free, 1)
                        if prev and GELU_AT[h] == t:
                            landed = {}
                            for u in range(PAIRS):
                                bank, before = banks.of(ph, ("fc1", PAIRS * h + u), turn)
                                landed[bank] = before + 1
                            for bank, count in landed.items():
                                act.wait_ge(lin_free[bank], count)
                            for c in range(3):
                                part = uf[:, 3 * HALF * c:3 * HALF * (c + 1)]
                                fn(part, part, gelu[ph.prev_layer]).then_inc(gelu_done, 1)

            for ph in PHASES:
                if ph.times == 1:
                    step(ph, ph.first, None, 0)
                else:
                    first = ph.first - BATCH * ph.base
                    with act.Fori(first, first + ph.times) as b:
                        step(ph, b + BATCH * ph.base, b, b - first)

        @block.vector
        def _(dve):
            v = nc.vector
            v.memset(neghalf[:, :], -0.5)
            v.memset(v_next[:, :, :], 0.0).then_inc(const_set, 1)
            dve.wait_ge(const_set, 1)
            v.memset(v_next[:, :, 0:HEADS * VW].rearrange("p t (h d) -> p t h d", d=VW)[:, :, :, HD:VW], 1.0).then_inc(const_set, 1)
            dve.wait_ge(cond_exp, 1)
            v.tensor_scalar(csil[:, 2, :], csil[:, 1, :], 1.0, None, ALU.add).then_inc(cond_step, 1)
            dve.wait_ge(cond_step, 1)
            v.reciprocal(csil[:, 1, :], csil[:, 2, :]).then_inc(cond_step, 1)
            dve.wait_ge(cond_step, 2)
            v.tensor_tensor(csil[:, 3, :], csil[:, 0, :], csil[:, 1, :], ALU.mult).then_inc(cond_step, 1)
            dve.wait_ge(cond_tr, 1)
            v.tensor_copy(csil_t[:, 0:2, :], lin_ps[0][:, 0:2 * BATCH].rearrange("p (k b) -> p k b", b=BATCH))
            v.tensor_copy(csil_t[0:TAIL, 2, :], lin_ps[0][0:TAIL, 2 * BATCH:3 * BATCH]).then_inc(cond_step, 1)
            def keep_prm(layer):
                rows = (6, 10)[layer]
                dve.wait_ge(prm_tr, layer + 1)
                v.tensor_copy(prm_t[:, layer, 0:2, 0:rows],
                              lin_ps[1 - layer][:, 0:32].rearrange("p (k r) -> p k r", r=16)[:, :, 0:rows])
                v.tensor_copy(prm_t[0:3 * TAIL, layer, 2, 0:rows],
                              lin_ps[1 - layer][0:3 * TAIL, 32:32 + rows]).then_inc(prm_done, 1)

            keep_prm(0)

            def ada_out(n, ps, out):
                layer, ch = divmod(n, 6)
                norm = ch // 3
                if ch % 3 == 2:
                    dve.wait_ge(ada_bias_in, 48 * (layer + 1))
                    if layer:
                        dve.wait_ge(gate_out, 16)
                    v.tensor_tensor(gate_sb[:, norm, :], ps[0:BATCH, 0:C], gate_bias[:, norm, :], ALU.add).then_inc(out, 1)
                    return
                dve.wait_ge(prm_done, layer + 1)
                dst = mod_b if ch % 3 == 0 else mod_a
                for f in range(3):
                    r = P if f < 2 else 3 * TAIL
                    last = v.tensor_scalar(dst[0:r, layer, norm, f, :], ps[0:r, BATCH * f:BATCH * (f + 1)],
                                           prm_t[0:r, layer, f, ch:ch + 1], float(ch % 3), ALU.add, ALU.add)
                last.then_inc(out, 1)

            for n in range(ADA_HEAD):
                dve.wait_ge(ada_mm, n + 1)
                ada_out(n, lin_ps[2], ada_vec)
            dve.wait_ge(const_in, 32)

            def split_chunk(chunk):
                kind, dst, k, cols, _, bias = weight_chunk(chunk)
                dve.wait_ge(w_in[chunk % 2] if chunk >= CH_QKV else w_first_in, chunk_in(chunk))
                if not is_tail(chunk):
                    high = dst[:, 0, k, :] if kind == "f" else dst[:, k, cols]
                    v.tensor_copy(high, stage(chunk)).then_inc(w_high, 1)
                    return
                rows = 3 * TAIL + (2 if bias is not None else 0)
                if bias is None:
                    v.memset(dst[3 * TAIL:KT_TAIL, 4, cols].bitcast(F32), 0.0)
                stacked = dst[0:rows, 4, cols]
                v.tensor_copy(stacked, stage(chunk)[0:rows, :]).then_inc(w_high, 1)
                dve.wait_ge(w_high, chunk + 1)
                v.scalar_tensor_tensor(out=stacked, in0=stacked.bitcast(F32), scalar=lomask[0:rows, 0:1],
                                       in1=stage(chunk)[0:rows, :], op0=ALU.mult, op1=ALU.add).then_inc(w_tail, 1)

            def step(ph, n, b, turn):
                attn, prev, nxt = ph.attn, ph.prev, ph.nxt
                A, Q, R, L = ph.counts(n)
                A2, Q2, R2 = A + 1 if attn else A, Q + 1 if prev else Q, R + 1 if nxt else R
                x_of = (x_pre, x_post)

                def bank_of(unit):
                    bank, before = banks.of(ph, unit, turn)
                    dve.wait_ge(lin_done[bank], before + 1)
                    return lin_ps[bank], lin_free[bank]

                def released(unit):
                    bank, before = banks.of(ph, unit, turn)
                    dve.wait_ge(lin_free[bank], before + 1)

                def norm(kind, part):
                    m = (L, Q)[kind]
                    layer = (ph.norm_layer, ph.prev_layer)[kind]
                    x, st, avg = x_of[kind], stats[:, kind, :, :], mv[:, kind, :, :]
                    if part == 0:
                        if kind == 0:
                            dve.wait_ge(xpre_in, 16 * (L + 1))
                        else:
                            dve.wait_ge(x1_done, TT * (Q + 1))
                    if part in (0, 1):
                        for tt in (2 * part, 2 * part + 1):
                            last = v.bn_stats(st[:, tt, :], x[:, tt, :])
                        if part == 1:
                            last.then_inc(stat_done[kind], 1)
                    if part == 2:
                        dve.wait_ge(const_in, 32)
                        dve.wait_ge(stat_done[kind], m + 1)
                        for tt in range(TT):
                            last = v.bn_aggr(avg[:, tt, :], st[:, tt, :])
                        last.then_inc(mv_done[kind], 1)
                        dve.wait_ge(mv_done[kind], m + 1)
                        v.tensor_scalar(veps[:, kind, :], avg[:, :, 1], EPS[layer], None, ALU.add).then_inc(veps_done[kind], 1)
                    if part == 3:
                        dve.wait_ge(rstd_done[kind], m + 1)
                        wait(dve, hi_done[0], 3 * R2)
                        if kind == 0:
                            wait(dve, hi_done[1], 3 * Q2)
                    if part in (3, 4):
                        for tt in (2 * (part - 3), 2 * (part - 3) + 1):
                            last = v.tensor_scalar(xn[:, tt, 0:C], x[:, tt, :], avg[:, tt, 0:1], rstd[:, kind, tt:tt + 1],
                                                   ALU.subtract, ALU.mult)
                        if part == 4:
                            last.then_inc(norm_done[kind], 1)
                    if part == 5:
                        dve.wait_ge(norm_done[kind], m + 1)
                        repeat_tail(xn).then_inc(xn_ready[kind], 1)

                def repeat_tail(x):
                    return v.tensor_copy(x[:, :, C:CREP].rearrange("p t (a n) -> p t a n", n=TAIL),
                                         x[:, :, None, 2 * P:C].to_broadcast([P, TT, 2, TAIL]))

                def halves(kind, t, at, low_at):
                    m = (R, Q)[kind]
                    tiles = [hpre_main[:, 0, :], hpre_main[:, 1, :], hpre_tail[0:3 * TAIL, :]] if kind == 0 else \
                        [hpost[:, 0, :], hpost[:, 1, :], hpost[0:3 * TAIL, 4, :]]
                    for f in range(3):
                        if at[f] == t:
                            released((("trpre", "trpost")[kind], f))
                            rows = P if f < 2 else 3 * TAIL
                            v.tensor_copy(tiles[f], hf[f][0:rows, :]).then_inc(hi_done[kind], 1)
                    if low_at[0] == t:
                        low = hpre_main[:, 3, :] if kind == 0 else hpost[:, 3, :]
                        dve.wait_ge(hi_done[kind], 3 * (m + 1))
                        v.tensor_tensor(low, hf[1], tiles[1].bitcast(F32), ALU.subtract).then_inc(lo_dve[kind], 1)
                    if low_at[1] == t:
                        mid = tiles[2][TAIL:2 * TAIL, :]
                        v.tensor_tensor(mid, hf[2][TAIL:2 * TAIL, :], mid.bitcast(F32), ALU.subtract).then_inc(lo_dve[kind], 1)

                def split_hidden(h, c):
                    part = uf[:, 3 * HALF * c:3 * HALF * (c + 1)].rearrange("p (f n) -> p f n", n=HALF)
                    return hid[:, 0, 3 * c:3 * c + 3, :], hid[:, 1, 3 * c:3 * c + 3, :], part

                def rest_of_ada(n):
                    layer, ch = divmod(n, 6)
                    norm = ch // 3
                    ps, free = bank_of(("ada", n))
                    ada_out(n, ps, free)
                    if ch == 5:
                        released(("ada", n))
                        v.tensor_tensor(gate_sb[:, 2, :], gate_sb[:, 1, :], gate_bias[:, 2, :], ALU.mult).then_inc(gate_step, 1)
                    if layer and ch % 3 == 1:
                        released(("ada", n))
                        for f in range(3):
                            r = P if f < 2 else 3 * TAIL
                            a, bb = mod_a[0:r, layer, norm, f, :], mod_b[0:r, layer, norm, f, :]
                            last = v.scalar_tensor_tensor(out=bb, in0=a, scalar=prm_t[0:r, layer, f, 7 + 2 * norm:8 + 2 * norm],
                                                          in1=bb, op0=ALU.mult, op1=ALU.add)
                        last.then_inc(mod_step, 1)
                        dve.wait_ge(mod_step, 2 * norm + 1)
                        for f in range(3):
                            r = P if f < 2 else 3 * TAIL
                            a = mod_a[0:r, layer, norm, f, :]
                            last = v.tensor_scalar(a, a, prm_t[0:r, layer, f, 6 + 2 * norm:7 + 2 * norm], None, ALU.mult)
                        last.then_inc(mod_step, 1)

                for t in range(NS):
                    s = t + AHEAD
                    if attn if s < NS else nxt:
                        g1, l1, n1 = (s // 16) % GROUPS, s % 16, (A if s < NS else R)
                        dve.wait_ge(s1_done, NS * n1 + s % NS + 1)
                        v.tensor_reduce(mx[:, g1, l1:l1 + 1], s1_ps[s % 2][:, :], AX.X, ALU.max, negate=True).then_inc(mx_done, 1)
                    if ph.ada and t - 1 in ADA_AT:
                        rest_of_ada(ADA_HEAD + ADA_AT.index(t - 1))
                    for at, chunk in RELOAD.get(ph.name, ()):
                        if at == t:
                            if chunk == N_CHUNKS + AT_FC1:
                                released(("fc1", 2 * PAIRS - 1))
                            split_chunk(chunk)
                    for part in range(6):
                        if ph.norm and LN1_AT[part] == t:
                            norm(0, part)
                    if t == VCUR_AT and attn:
                        wait(dve, pv_done, 16 * A)
                        for bank in range(NLIN):
                            wait(dve, lin_free[bank], banks.before(ph, bank, turn))
                        v.tensor_copy(v_cur[:, :, :], v_next[:, :, :]).then_inc(vcur_ready, 1)
                    if nxt:
                        halves(0, t, PRE_HI_AT, PRE_LO_AT)
                    if t % 16 == OT_AT[2] and (prev if t < 16 else attn):
                        og, n1 = (t // 16 - 1) % GROUPS, A - (t < 16)
                        ps, free = bank_of(("ot", og))
                        o = ps[:, :].rearrange("p (t h c) -> p t h c", t=TT, c=32)
                        v.reciprocal(osum[:, :, :, :], o[:, :, :, HD:HD + 1]).then_inc(osum_done, 1)
                        dve.wait_ge(osum_done, GROUPS * n1 + og + 1)
                        if og == 0:
                            wait(dve, tro_hi, 3 * Q2)
                        dst = on[:, :, GROUP * HD * og:GROUP * HD * (og + 1)].rearrange("p t (h d) -> p t h d", d=HD)
                        v.tensor_tensor(dst, o[:, :, :, 0:HD], osum[:, :, :, :].to_broadcast([P, TT, GROUP, HD]),
                                        ALU.mult).then_inc(free, 1)
                        if og == GROUPS - 1:
                            released(("ot", og))
                            repeat_tail(on).then_inc(on_ready, 1)
                    if t % 16 == MX_AT[1] and (attn if t < 48 else nxt):
                        g1, n1 = (t // 16 + 1) % GROUPS, (A if t < 48 else R)
                        ps, free = bank_of(("mx", g1))
                        k = GROUPS * n1 + g1 + 1
                        wait(dve, mx_in[g1], 16 * n1)
                        v.tensor_copy(mx_part[:, g1, 0, :], ps[0:16, 0:P]).then_inc(mxh_done, 1)
                        dve.wait_ge(mxh_done, k)
                        v.tensor_tensor(mx_rest[:, g1, :], ps[0:16, 0:P], mx_part[:, g1, 0, :], ALU.subtract).then_inc(free, 1)
                        released(("mx", g1))
                        v.tensor_copy(mx_part[:, g1, 1, :], mx_rest[:, g1, :]).then_inc(mxm_done, 1)
                        dve.wait_ge(mxm_done, k)
                        v.tensor_tensor(mx_part[:, g1, 2, :], mx_rest[:, g1, :], mx_part[:, g1, 1, :], ALU.subtract).then_inc(mxl_done, 1)
                    for f in range(3):
                        if prev and TRO_LO_AT[f] == t:
                            ps, free = bank_of(("tro", f))
                            dve.wait_ge(tro_hi, 3 * Q + f + 1)
                            if f < 2:
                                low, high, whole = hpost[:, 2 + f, :], hpost[:, f, :], ps[:, :]
                            else:
                                low = high = hpost[TAIL:2 * TAIL, 4, :]
                                whole = ps[TAIL:2 * TAIL, :]
                            v.tensor_tensor(low, whole, high.bitcast(F32), ALU.subtract).then_inc(free, 1)
                    for tt in range(TT):
                        if prev and PROJ_OUT_AT[tt] == t:
                            ps, free = bank_of(("proj", tt))
                            if tt == 0:
                                dve.wait_ge(gates_in, 16 * (Q + 1))
                            if tt < 2:
                                wait(dve, x2_done, TT * Q)
                            else:
                                dve.wait_ge(x1_done, TT * Q + tt - 1)
                            v.tensor_tensor(gated[:, tt % 2, :], ps[:, 0:C], gates[:, 0, :], ALU.mult).then_inc(free, 1)
                    for m in range(QK_TILES):
                        if nxt and QK_OUT_AT[m] == t:
                            ps, free = bank_of(("qk", m))
                            rows = QK_ROWS[m]
                            dve.wait_ge(qkh_done, QK_TILES * R + m + 1)
                            wait(dve, qkl_done, QK_TILES * R + m - 1)
                            v.tensor_tensor(rr[m % 2][0:rows, :], ps[0:rows, :], qk_part[0:rows, m % 2, 0, :],
                                            ALU.subtract).then_inc(free, 1)
                    for part in range(6):
                        if prev and LN2_AT[part] == t:
                            norm(1, part)
                    if prev:
                        halves(1, t, POST_HI_AT, POST_LO_AT)
                    for h in range(2):
                        for c in range(3):
                            if prev and SPLIT_AT[h][c] == t:
                                if h == 0 and c == 0 and nxt:
                                    released(("v", TT - 1))
                                high, low, part = split_hidden(h, c)
                                dve.wait_ge(gelu_done, 6 * Q + 3 * h + c + 1)
                                v.tensor_copy(high, part).then_inc(ghi_done, 1)
                                if c < 2:
                                    dve.wait_ge(ghi_done, 6 * Q + 3 * h + c + 1)
                                    v.tensor_tensor(low, part, high.bitcast(F32), ALU.subtract).then_inc(glo_dve, 1)
                        for i in range(2):
                            if prev and FC2_OUT_AT[2 * h + i] == t:
                                k = 2 * h + i
                                ps, free = bank_of(("fc2", k))
                                if k < 2:
                                    dve.wait_ge(x1_done, TT * (Q + 1))
                                else:
                                    dve.wait_ge(x2_done, TT * Q + k - 1)
                                v.tensor_tensor(gated[:, k % 2, :], ps[:, 0:C], gates[:, 1, :], ALU.mult).then_inc(free, 1)

            for ph in PHASES:
                if ph.times == 1:
                    step(ph, ph.first, None, 0)
                else:
                    first = ph.first - BATCH * ph.base
                    with dve.Fori(first, first + ph.times) as b:
                        step(ph, b + BATCH * ph.base, b, b - first)
                if ph.name == "start":
                    for chunk in range(CH_QKV):
                        split_chunk(chunk)
                    keep_prm(1)

        @block.gpsimd
        def _(pool):
            g = nc.gpsimd
            g.memset(hpre_tail[96:P, :].bitcast(F32), 1.0)
            g.memset(hpost[96:P, 4, :].bitcast(F32), 1.0)
            g.memset(k_stack[96:P, :, :, :], 1.0).then_inc(ones_set, 1)
            pool.wait_ge(ones_set, 1)
            pool.wait_ge(const_set, 1)

            def split_chunk(chunk):
                if is_tail(chunk):
                    return
                kind, dst, k, cols, _, _ = weight_chunk(chunk)
                high, low = (dst[:, 0, k, :], dst[:, 1, k, :]) if kind == "f" else (dst[:, k, cols], dst[:, 2 + k, cols])
                pool.wait_ge(w_high, chunk + 1)
                g.tensor_tensor(low, stage(chunk), high.bitcast(F32), ALU.subtract).then_inc(w_low, 1)

            def step(ph, n, b, turn):
                attn, prev, nxt = ph.attn, ph.prev, ph.nxt
                A, Q, R, L = ph.counts(n)

                def released(unit):
                    bank, before = banks.of(ph, unit, turn)
                    pool.wait_ge(lin_free[bank], before + 1)

                def inverse_root(kind):
                    pool.wait_ge(veps_done[kind], (L, Q)[kind] + 1)
                    g.tensor_tensor(rstd[:, kind, :], veps[:, kind, :], neghalf[:, :], ALU.pow).then_inc(rstd_done[kind], 1)

                def low_half(kind):
                    pool.wait_ge(hi_done[kind], 3 * (R, Q)[kind] + 1)
                    high, low = (hpre_main[:, 0, :], hpre_main[:, 2, :]) if kind == 0 else (hpost[:, 0, :], hpost[:, 2, :])
                    g.tensor_tensor(low, hf[0], high.bitcast(F32), ALU.subtract).then_inc(lo_pool[kind], 1)

                for t in range(NS):
                    for at, chunk in RELOAD.get(ph.name, ()):
                        if at == t:
                            split_chunk(chunk)
                    if ph.norm and LN1_AT[2] == t:
                        inverse_root(0)
                    if nxt and PRE_HI_AT[0] == t:
                        low_half(0)
                    for tt in range(TT):
                        if prev and PROJ_OUT_AT[tt] == t:
                            if tt == 0:
                                pool.wait_ge(xpost_in, 16 * (Q + 1))
                            released(("proj", tt))
                            g.tensor_tensor(x_post[:, tt, :], x_post[:, tt, :], gated[:, tt % 2, :], ALU.add).then_inc(x1_done, 1)
                    for m in range(QK_TILES):
                        if nxt and QK_OUT_AT[m] == t:
                            rows = QK_ROWS[m]
                            pool.wait_ge(qkm_done, QK_TILES * R + m + 1)
                            g.tensor_tensor(qk_part[0:rows, m % 2, 2, :], rr[m % 2][0:rows, :], qk_part[0:rows, m % 2, 1, :],
                                            ALU.subtract).then_inc(qkl_done, 1)
                    if prev and LN2_AT[2] == t:
                        inverse_root(1)
                    if prev and POST_HI_AT[0] == t:
                        low_half(1)
                    if prev and t == BIAS_AT:
                        pool.wait_ge(norm_done[1], Q + 1)
                        pool.wait_ge(gates_in, 16 * (Q + 1))
                        g.tensor_tensor(x_post[:, :, :], x_post[:, :, :], gates[:, 2:3, :].to_broadcast([P, TT, C]),
                                        ALU.add).then_inc(gb_done, 1)
                    for h in range(2):
                        if prev and SPLIT_AT[h][2] == t:
                            pool.wait_ge(ghi_done, 6 * Q + 3 * h + 3)
                            part = uf[:, 6 * HALF:9 * HALF].rearrange("p (f n) -> p f n", n=HALF)
                            g.tensor_tensor(hid[:, 1, 6:9, :], part, hid[:, 0, 6:9, :].bitcast(F32), ALU.subtract).then_inc(glo_pool, 1)
                        for i in range(2):
                            if prev and FC2_OUT_AT[2 * h + i] == t:
                                k = 2 * h + i
                                released(("fc2", k))
                                pool.wait_ge(gb_done, Q + 1)
                                g.tensor_tensor(x_post[:, k, :], x_post[:, k, :], gated[:, k % 2, :], ALU.add).then_inc(x2_done, 1)

            for ph in PHASES:
                if ph.times == 1:
                    step(ph, ph.first, None, 0)
                else:
                    first = ph.first - BATCH * ph.base
                    with pool.Fori(first, first + ph.times) as b:
                        step(ph, b + BATCH * ph.base, b, b - first)
                if ph.name == "start":
                    for chunk in range(CH_QKV):
                        split_chunk(chunk)


_INS = ['x', 'cond_1152', 'L0_cond_W_qkv', 'L0_cond_b_qkv', 'L0_cond_W_proj', 'L0_cond_b_proj', 'L0_cond_W_fc1',
        'L0_cond_b_fc1', 'L0_cond_W_fc2', 'L0_cond_b_fc2', 'L0_cond_W_ada', 'L0_cond_b_ada', 'L1_cond_ln1_w',
        'L1_cond_ln1_b', 'L1_cond_wq', 'L1_cond_wk', 'L1_cond_wv', 'L1_cond_wo', 'L1_cond_wo_b', 'L1_cond_ln2_w',
        'L1_cond_ln2_b', 'L1_cond_fc1_w', 'L1_cond_fc1_b', 'L1_cond_fc2_w', 'L1_cond_fc2_b', 'L1_cond_ada_w',
        'L1_cond_ada_b']


def kernel(**inputs):
    import numpy as _np
    import concourse.bacc as _bacc
    from concourse import mybir as _mybir
    from concourse.bass_utils import run_bass_kernel_spmd as _run

    nc = _bacc.Bacc("TRN2", target_bir_lowering=False, num_devices=1)
    arrays, ap = {}, {}

    def give(name, a):
        arrays[name] = _np.ascontiguousarray(a)
        ap[name] = nc.dram_tensor(name, arrays[name].shape, _mybir.dt.from_np(arrays[name].dtype), kind="ExternalInput").ap()

    for name in _INS:
        give(name, inputs[name])
    give("ident_const", _np.eye(P, dtype=_np.float32))
    low_rows = _np.zeros((P, 1), _np.float32)
    low_rows[2 * TAIL:3 * TAIL] = -1.0
    low_rows[3 * TAIL + 1] = -1.0
    give("low_rows_const", low_rows)
    out = nc.dram_tensor("out_dram", (BATCH, TOK, C), _mybir.dt.float32, kind="ExternalOutput").ap()
    a, b = "L0_cond_", "L1_cond_"
    weights = (
        dict(qkv=[ap[a + "W_qkv"]], b_qkv=ap[a + "b_qkv"], proj=ap[a + "W_proj"], b_proj=ap[a + "b_proj"],
             fc1=ap[a + "W_fc1"], b_fc1=ap[a + "b_fc1"], fc2=ap[a + "W_fc2"], b_fc2=ap[a + "b_fc2"],
             ada=ap[a + "W_ada"], b_ada=ap[a + "b_ada"], ln=[]),
        dict(qkv=[ap[b + "wq"], ap[b + "wk"], ap[b + "wv"]], b_qkv=None, proj=ap[b + "wo"], b_proj=ap[b + "wo_b"],
             fc1=ap[b + "fc1_w"], b_fc1=ap[b + "fc1_b"], fc2=ap[b + "fc2_w"], b_fc2=ap[b + "fc2_b"],
             ada=ap[b + "ada_w"], b_ada=ap[b + "ada_b"],
             ln=[ap[b + n] for n in ("ln1_w", "ln1_b", "ln2_w", "ln2_b")]),
    )
    two_layer_block(nc, ap["x"], ap["cond_1152"], ap["low_rows_const"], ap["ident_const"], weights, out)
    r = _run(nc, [arrays], core_ids=[0])
    return r.results[0]["out_dram"]
```
